# Optimizing a Trainium2 kernel written in Bass

```python
import numpy as np
import jax
import jax.numpy as jnp

def _softmax(x, axis=-1):
    return jax.nn.softmax(x, axis=axis)

def _gelu(x):
    return jax.nn.gelu(x, approximate=True)

def _silu(x):
    return jax.nn.silu(x)

def _sigmoid(x):
    return jax.nn.sigmoid(x)

def _layernorm(x, axis=-1, eps=1e-05):
    m = jnp.mean(x, axis=axis, keepdims=True)
    v = jnp.var(x, axis=axis, keepdims=True)
    return (x - m) / jnp.sqrt(v + eps)

def _scatter_add(tgt, idx, src, axis=0):
    return tgt.at[idx].add(src)

def _segment_sum(src, seg, n):
    return jax.ops.segment_sum(src, seg, n)
kernel_name = 'mk_gnn_ffn_d1_gnn_r8_6fe119'

def setup_inputs(seed: int=0):
    np.random.seed(seed)
    _w = jnp.asarray

    def _rec_inputs():
        import jax
        import jax.numpy as jnp
        _gk = jax.random.key(seed)
        x = -0.0002117 + 1 * jax.random.normal(jax.random.fold_in(_gk, 1), (6250, 256), jnp.float32)
        src = jax.random.randint(jax.random.fold_in(_gk, 2), (200000,), 0, 6250, jnp.int32)
        dst = jax.random.randint(jax.random.fold_in(_gk, 3), (200000,), 0, 6250, jnp.int32)
        _o = jnp.argsort(dst, stable=True)
        src = src[_o]
        dst = dst[_o]
        edge_attr_2 = jax.random.uniform(jax.random.fold_in(_gk, 11), (200000, 2), jnp.float32, 0.0, 1)
        return (x, src, dst, edge_attr_2)
    x, src, dst, edge_attr_2 = _rec_inputs()

    def _L0_gnn_setup():
        import jax, jax.numpy as jnp
        import numpy as np
        N_NODES = 12500
        N_EDGES = 200000
        IN_FEATS = 256
        OUT_FEATS = 64
        NUM_HEADS = 4
        key = jax.random.key(seed)
        k_h, k_adj, k_dir, k_wf, k_wr, k_af = jax.random.split(key, 6)
        h = jax.random.normal(k_h, (N_NODES, IN_FEATS), dtype=jnp.float32)
        adj = jax.random.randint(k_adj, (2, N_EDGES), 0, N_NODES, dtype=jnp.int64)
        bit = jax.random.randint(k_dir, (N_EDGES,), 0, 2).astype(jnp.float32)
        direction = jnp.stack([bit, 1.0 - bit], axis=1)
        s_w = float(np.sqrt(6.0 / (IN_FEATS + OUT_FEATS)))
        s_a = float(np.sqrt(6.0 / (NUM_HEADS + OUT_FEATS)))
        W_forward = jax.random.uniform(k_wf, (OUT_FEATS, IN_FEATS), jnp.float32, -s_w, s_w)
        W_reverse = jax.random.uniform(k_wr, (OUT_FEATS, IN_FEATS), jnp.float32, -s_w, s_w)
        attn_forward = jax.random.uniform(k_af, (1, NUM_HEADS, OUT_FEATS), jnp.float32, -s_a, s_a)
        return {'h': h, 'adj': adj, 'direction': direction, 'W_forward': W_forward, 'W_reverse': W_reverse, 'attn_forward': attn_forward}
    _L0_gnn_all = _L0_gnn_setup()
    _L0_gnn_in = {k: v for k, v in _L0_gnn_all.items() if k in ('W_forward', 'W_reverse', 'attn_forward')}
    del _L0_gnn_all

    def _L0_ffn_setup():
        import jax, jax.numpy as jnp
        import numpy as np
        B, S, H, F, E, K = (8, 512, 256, 512, 16, 2)
        EPS = 1e-05
        key = jax.random.key(seed)
        ks = jax.random.split(key, 9)
        sc = 0.02
        return {'x': jax.random.normal(ks[0], (B, S, H), dtype=jnp.float32), 'gate_w': jax.random.normal(ks[1], (H, E), dtype=jnp.float32) * sc, 'gate_b': jnp.zeros((E,), dtype=jnp.float32), 'w1': jax.random.normal(ks[2], (E, H, F), dtype=jnp.float32) * sc, 'b1': jnp.zeros((E, F), dtype=jnp.float32), 'w2': jax.random.normal(ks[3], (E, F, H), dtype=jnp.float32) * sc, 'b2': jnp.zeros((E, H), dtype=jnp.float32), 'gamma': jnp.ones((H,), dtype=jnp.float32), 'beta': jnp.zeros((H,), dtype=jnp.float32)}
    _L0_ffn_all = _L0_ffn_setup()
    _L0_ffn_in = {k: v for k, v in _L0_ffn_all.items() if k in ('gate_w', 'gate_b', 'w1', 'b1', 'w2', 'b2', 'gamma', 'beta')}
    del _L0_ffn_all
    return {'x': x, 'src': src, 'dst': dst, 'edge_attr_2': edge_attr_2, 'L0_gnn_W_forward': _L0_gnn_in['W_forward'], 'L0_gnn_W_reverse': _L0_gnn_in['W_reverse'], 'L0_gnn_attn_forward': _L0_gnn_in['attn_forward'], 'L0_ffn_gate_w': _L0_ffn_in['gate_w'], 'L0_ffn_gate_b': _L0_ffn_in['gate_b'], 'L0_ffn_w1': _L0_ffn_in['w1'], 'L0_ffn_b1': _L0_ffn_in['b1'], 'L0_ffn_w2': _L0_ffn_in['w2'], 'L0_ffn_b2': _L0_ffn_in['b2'], 'L0_ffn_gamma': _L0_ffn_in['gamma'], 'L0_ffn_beta': _L0_ffn_in['beta']}

def reference(x, src, dst, edge_attr_2, L0_gnn_W_forward, L0_gnn_W_reverse, L0_gnn_attn_forward, L0_ffn_gate_w, L0_ffn_gate_b, L0_ffn_w1, L0_ffn_b1, L0_ffn_w2, L0_ffn_b2, L0_ffn_gamma, L0_ffn_beta):
    import jax
    import jax.numpy as jnp

    def _L0_gnn_ref(h, adj, direction, W_forward, W_reverse, attn_forward):
        import jax, jax.numpy as jnp
        import numpy as np
        N_NODES = 12500
        N_EDGES = 200000
        IN_FEATS = 256
        OUT_FEATS = 64
        NUM_HEADS = 4
        N = h.shape[0]
        H = attn_forward.shape[1]
        h_fwd = h @ W_forward.T
        h_rev = h @ W_reverse.T
        src, dst = (adj[0], adj[1])
        messages = h_fwd[src] * direction[:, 0:1] + h_rev[src] * direction[:, 1:2]
        scores = jnp.einsum('ef,hf->eh', messages, attn_forward[0])
        scores = jax.nn.leaky_relu(scores, negative_slope=0.2)
        exp_scores = jnp.exp(scores - scores.max(axis=0, keepdims=True))
        sum_exp = jax.ops.segment_sum(exp_scores, dst, num_segments=N)
        norm = exp_scores / (sum_exp[dst] + 1e-10)
        outs = [jax.ops.segment_sum(messages * norm[:, hd:hd + 1], dst, num_segments=N) for hd in range(H)]
        out = jnp.stack(outs, axis=1)
        return out.reshape(N, -1)

    def _L0_ffn_ref(x, gate_w, gate_b, w1, b1, w2, b2, gamma, beta):
        import jax, jax.numpy as jnp
        import numpy as np
        B, S, H, F, E, K = (8, 512, 256, 512, 16, 2)
        EPS = 1e-05
        gate_logits = x @ gate_w + gate_b
        topk_vals, topk_idx = jax.lax.top_k(gate_logits, K)
        topk_w = jax.nn.softmax(topk_vals, axis=-1)
        h = jax.nn.relu(jnp.einsum('bsh,ehf->bsef', x, w1) + b1)
        expert_out = jnp.einsum('bsef,efh->bseh', h, w2) + b2
        sel = jnp.take_along_axis(expert_out, topk_idx[:, :, :, None], axis=2)
        moe = jnp.sum(topk_w[..., None] * sel, axis=2)
        y = x + moe
        mu = jnp.mean(y, axis=-1, keepdims=True)
        var = jnp.var(y, axis=-1, keepdims=True)
        return (y - mu) / jnp.sqrt(var + EPS) * gamma + beta
    edge_index = jnp.stack([src, dst])
    x = x + _L0_gnn_ref(_layernorm(x, axis=-1), edge_index, edge_attr_2, L0_gnn_W_forward, L0_gnn_W_reverse, L0_gnn_attn_forward)
    x = x + _L0_ffn_ref(_layernorm(x, axis=-1)[None], L0_ffn_gate_w, L0_ffn_gate_b, L0_ffn_w1, L0_ffn_b1, L0_ffn_w2, L0_ffn_b2, L0_ffn_gamma, L0_ffn_beta)[0]
    return x

_drawn_inputs = setup_inputs


def setup_inputs(seed=0):
    import zlib

    import numpy as np

    out = dict(_drawn_inputs(seed))
    spreads = {'L0_ffn_gate_b': (0.0, 0.1),
     'L0_ffn_b1': (0.0, 0.759),
     'L0_ffn_b2': (0.0, 0.1),
     'L0_ffn_gamma': (1.0, 0.2),
     'L0_ffn_beta': (0.0, 0.1)}
    factors = {}
    for name, (base, spread) in spreads.items():
        noise = np.random.default_rng([zlib.crc32(name.encode()), seed]).standard_normal(out[name].shape)
        drawn = base * np.exp(spread * noise) if base else spread * noise
        out[name] = jnp.asarray(drawn.astype(out[name].dtype))
    for name, factor in factors.items():
        out[name] = (out[name] * factor).astype(out[name].dtype)
    return out
```

```python
from contextlib import ExitStack

import concourse.bass as bass
from concourse import mybir

F32 = mybir.dt.float32
BF16 = mybir.dt.bfloat16
I32 = mybir.dt.int32
U32 = mybir.dt.uint32
ALU = mybir.AluOpType
ACT = mybir.ActivationFunctionType
AX = mybir.AxisListType
ds = bass.ds

P = 128
N = 6250
D = 256
HD = 64
HEADS = 4
NT = -(-N // P)
NP = NT * P
LAST = N - (NT - 1) * P
U = 7
NG = NT // U
assert NG * U == NT

EDGES = 200000
K = 8
CHUNK = K * P
RING = 4
NCH = -(-EDGES // (CHUNK * RING)) * RING
NIT = NCH // RING
W = 64
WSH = 6
EXTRA = 8192
MAXWIN = NP // W
COLS = HD + HEADS
ROW = 2 * COLS
NCB = NCH // 2
assert NCB <= P

E = 16
F = 512
KC = D // P
FC = F // P
NJ = (2 * N + E * (P - 1)) // P + 1
NJ += NJ % 2
SLOTS = NJ * P
XROW = D + 2
G2 = 2 * NT
FAR = 1.0e6
LN_EPS = 1e-5
HEADROOM = 40.0


def after(eng, sem, count):
    if isinstance(count, int) and count <= 0:
        return
    eng.wait_ge(sem, count)


def settle(eng, turns):
    eng.sem_inc(turns, 1)


def reuse(u, depth, unroll):
    d = 1
    while ((u - d) % unroll) % depth != u % depth:
        d += 1
    return d


def groups(eng, step, last_apart=True):
    step(0)
    with eng.Fori(1, NG - 1) as i:
        step(i)
    step(NG - 1)


def build(nc, x, src, dst, attr, w_fwd, w_rev, w_fwd_t, w_rev_t, attn_t, gate_w, gate_b,
          w1, b1, w2, b2, gamma, beta, out):
    table = nc.dram_tensor("node_table", (NP, ROW), F32).ap()
    dispatched = nc.dram_tensor("dispatched", (SLOTS, XROW), F32).ap()
    expert_rows = nc.dram_tensor("expert_rows", (2 * NP, D), F32).ap()
    residual = nc.dram_tensor("residual", (NP, D), F32).ap()

    with ExitStack() as whole:
        def tensors(ctx):
            def sb(name, shape, dt=F32):
                return ctx.enter_context(nc.sbuf_tensor(name, shape, dt))

            def ps(name, shape, dt=F32):
                return ctx.enter_context(nc.psum_tensor(name, shape, dt))

            def sem(name):
                return ctx.enter_context(nc.semaphore(name))
            return sb, ps, sem

        sb, _, _ = tensors(whole)
        ident = sb("ident", [P, P])
        ones = sb("ones", [P, P])
        eps = sb("eps", [P, 1])
        iota_w = sb("iota_w", [P, W])
        token_rows = sb("token_rows", [P, NT, XROW])
        top_w = sb("top_w", [P, NT, 2])
        slot_of = sb("slot_of", [P, NT, 2], I32)
        expert_f = sb("expert_f", [P, NJ])
        expert_of_tile = sb("expert_of_tile", [1, NJ], I32)

        with ExitStack() as graph:
            gsb, _, _ = tensors(graph)
            acc = gsb("acc", [P, 2, NP + W])
            acc_e = gsb("acc_e", [HEADS, NP + W])
            run_max = gsb("run_max", [P, K, HEADS])
            neg_shift = gsb("neg_shift", [P, 1])
            stage_edges(nc, tensors, locals())
            stage_nodes(nc, tensors, locals())
        with ExitStack() as moe:
            msb, _, _ = tensors(moe)
            stage_experts(nc, tensors, locals())


def stage_edges(nc, tensors, g):
    x, src, dst, attr, table, dispatched = (g[n] for n in ("x", "src", "dst", "attr", "table", "dispatched"))
    ident, ones, eps, iota_w, token_rows, acc, acc_e, run_max, neg_shift = (
        g[n] for n in ("ident", "ones", "eps", "iota_w", "token_rows", "acc", "acc_e", "run_max", "neg_shift"))
    with ExitStack() as edges:
        esb, _, _ = tensors(edges)
        attr_all = esb("attr_all", [P, 2, NCH * K])
        dst_rel = esb("dst_rel", [P, NCH * K])
        windows = esb("windows", [1, 1 + NCH], I32)
        pad_row = esb("pad_row", [P, XROW])
        before = esb("before", [1, NCH], I32)

        with ExitStack() as ctx:
            sb, ps, sem = tensors(ctx)
            dst_i = sb("dst_i", [P, NCH * K], I32)
            w_nat = sb("w_nat", [HD, 2, D])
            attn_sb = sb("attn_sb", [HD, HEADS])
            w_all = sb("w_all", [P, KC, ROW])
            stats = sb("stats", [P, U, 6])
            mv = sb("mv", [P, U, 2])
            rstd = sb("rstd", [P, U])
            xn = sb("xn", [P, U, D])
            xn_t = sb("xn_t", [P, 2, KC, P])
            tab = sb("tab", [P, U, ROW])
            tab_max = sb("tab_max", [P, 2, HEADS])
            ten = sb("ten", [P, 10])
            ten_max = sb("ten_max", [10, 1])
            lohi = sb("lohi", [P, 2, NCH])
            lohi_c = sb("lohi_c", [P, 4])
            row = sb("row", [1, 4, NCH])
            span = sb("span", [1, NCH], I32)
            small = sb("small", [1, 16])

            p_xt = ps("p_xt", [P, 2, 512])
            p_tab = ps("p_tab", [P, 2, 512])
            p_a = ps("p_a", [P, 512])
            p_b = ps("p_b", [P, 512])
            p_c = ps("p_c", [P, 512])
            p_d = ps("p_d", [P, 512])

            s_x = sem("x_loaded")
            s_edge = sem("edges_loaded")
            s_w = sem("weights_loaded")
            s_ident = sem("ident_ready")
            s_chain = sem("dve_steps")
            turns = sem("dve_turns")
            s_eps = sem("eps_ready")
            s_mv = sem("mean_var_ready")
            s_rstd = sem("rstd_ready")
            s_xn = sem("xn_ready")
            s_xt = sem("xn_transposed")
            s_xtc = sem("xn_t_copied")
            s_tab = sem("table_tile_done")
            s_tabc = sem("table_tile_copied")
            s_max = sem("table_max_taken")
            s_big = sem("group_max_taken")
            s_stored = sem("table_stored")
            s_ws = sem("score_weights_done")
            s_wsc = sem("score_weights_copied")
            s_lohi = sem("chunk_ranges")
            s_lohit = sem("chunk_ranges_transposed")
            s_lohic = sem("chunk_columns")
            s_rows = sem("chunk_rows")
            s_first = sem("first_row")
            s_firstb = sem("first_broadcast")
            s_ten = sem("maxima_columns")
            s_tent = sem("maxima_transposed")
            s_tenc = sem("maxima_reduced")
            s_tenr = sem("maxima_row")
            s_shift = sem("shift_value")
            s_shiftb = sem("shift_broadcast")
            s_init = sem("memory_set")

            with nc.Block() as block:
                @block.sync
                def _(sp):
                    for d, (nat, tr) in enumerate(((g["w_fwd"], g["w_fwd_t"]), (g["w_rev"], g["w_rev_t"]))):
                        sp.dma_start(w_nat[:, d, :], nat).then_inc(s_w, 16)
                        sp.dma_start(w_all[:, :, d * COLS:d * COLS + HD],
                                     tr.rearrange("(c p) f -> p c f", p=P)).then_inc(s_w, 16)
                    sp.dma_start(attn_sb[:, :], g["attn_t"]).then_inc(s_w, 16)
                    xv = x.rearrange("(g u p) d -> g p u d", p=P, u=U)
                    for i in range(NG):
                        sp.dma_start(token_rows[:, i * U:(i + 1) * U, 0:D], xv[i]).then_inc(s_x, 16)
                        if i == 0:
                            sp.dma_start(dst_i[:, :], dst).then_inc(s_edge, 16)
                            sp.dma_start(attr_all[:, :, :], attr).then_inc(s_edge, 16)
                        sp.wait_ge(s_x, 16 * (i + 1))

                @block.gpsimd
                def _(pool):
                    pool.memset(ident[:, :], 0.0).then_inc(s_init, 1)
                    pool.wait_ge(s_init, 1)
                    pool.affine_select(out=ident[:, :], in_=ident[:, :], compare_op=ALU.not_equal, fill=1.0,
                                       base=0, pattern=[[-1, P]], channel_multiplier=1).then_inc(s_ident, 1)
                    pool.memset(ones[:, :], 1.0).then_inc(s_ident, 1)
                    pool.iota(iota_w[:, :], pattern=[[1, W]], base=0, channel_multiplier=0,
                              allow_small_or_imprecise_dtypes=True).then_inc(s_ident, 1)
                    pool.memset(pad_row[:, :], 0.0).then_inc(s_init, 1)
                    pool.wait_ge(s_init, 2)
                    pool.memset(pad_row[:, D:D + 1], FAR)

                    pool.memset(acc_e[:, :], 0.0)
                    pool.memset(acc[:, :, :], 0.0)

                @block.scalar
                def _(act):
                    def copy(t, u):
                        act.wait_ge(s_xt, t + 1)
                        after(act, s_tab, t - reuse(u, 2, U) + 1)
                        act.activation(xn_t[:, u % 2, :, :], p_xt[:, u % 2, 0:D].rearrange("p (c n) -> p c n", c=KC),
                                       ACT.Copy).then_inc(s_xtc, 1)

                    def table_copy(t, u, i):
                        act.wait_ge(s_tab, t + 1)
                        if u == 0 and not (isinstance(i, int) and i == 0):
                            act.wait_ge(s_stored, i * 16)
                            act.wait_ge(s_max, i)
                        act.activation(tab[:, u, :], p_tab[:, u % 2, 0:ROW], ACT.Copy).then_inc(s_tabc, 1)

                    act.wait_ge(s_eps, 1)
                    tv = table.rearrange("(g u p) c -> g p u c", p=P, u=U)

                    def step(i):
                        act.wait_ge(s_mv, i + 1)
                        act.activation(rstd[:, :], mv[:, :, 1], ACT.Sqrt, bias=eps[:, 0:1]).then_inc(s_rstd, 1)
                        for u in range(U):
                            copy(i * U + u, u)
                            if u:
                                table_copy(i * U + u - 1, u - 1, i)
                        table_copy(i * U + U - 1, U - 1, i)
                        act.wait_ge(s_tabc, (i + 1) * U)
                        act.dma_start(tv[i] if isinstance(i, int) else
                                      tv[ds(i, 1)].rearrange("g p u c -> (g p) u c"), tab[:, :, :])\
                           .then_inc(s_stored, 16)
                    groups(act, step)
                    act.wait_ge(s_stored, NG * 16)

                @block.tensor
                def _(pe):
                    pe.wait_ge(s_w, 5 * 16)
                    for d in range(2):
                        for c in range(KC):
                            last = pe.matmul(p_a[:, (2 * d + c) * HEADS:(2 * d + c + 1) * HEADS],
                                             w_nat[:, d, c * P:(c + 1) * P], attn_sb[:, :], start=True, stop=True)
                    last.then_inc(s_ws, 1)
                    pe.wait_ge(s_ident, 3)

                    def transpose(t, u):
                        pe.wait_ge(s_xn, t + 1)
                        after(pe, s_xtc, t - reuse(u, 2, U) + 1)
                        for c in range(KC):
                            last = pe.transpose(p_xt[:, u % 2, c * P:(c + 1) * P], xn[:, u, c * P:(c + 1) * P],
                                                ident[:, :])
                        last.then_inc(s_xt, 1)

                    def product(t, u):
                        pe.wait_ge(s_xtc, t + 1)
                        if isinstance(t, int) and t == 0:
                            pe.wait_ge(s_wsc, 1)
                        after(pe, s_tabc, t - reuse(u, 2, U) + 1)
                        for c in range(KC):
                            last = pe.matmul(p_tab[:, u % 2, 0:ROW], xn_t[:, u % 2, c, :], w_all[:, c, :],
                                             start=(c == 0), stop=(c == KC - 1))
                        last.then_inc(s_tab, 1)

                    def step(i):
                        for u in range(U):
                            transpose(i * U + u, u)
                            if u:
                                product(i * U + u - 1, u - 1)
                        product(i * U + U - 1, U - 1)
                    groups(pe, step)

                    pe.wait_ge(s_lohi, 2)
                    for q in range(4):
                        last = pe.transpose(p_a[0:NCB, q * P:(q + 1) * P],
                                            lohi[:, q // 2, (q % 2) * NCB:(q % 2 + 1) * NCB], ident[:, :])
                    last.then_inc(s_lohit, 1)
                    pe.wait_ge(s_ten, 3)
                    pe.transpose(p_d[0:10, 0:P], ten[:, :], ident[:, :]).then_inc(s_tent, 1)
                    pe.wait_ge(s_lohic, 2)
                    for q in range(4):
                        last = pe.transpose(p_b[0:1, q * NCB:(q + 1) * NCB], lohi_c[0:NCB, q:q + 1],
                                            ident[0:NCB, 0:NCB])
                    last.then_inc(s_rows, 1)
                    pe.wait_ge(s_tenc, 1)
                    pe.transpose(p_d[0:1, P:P + 10], ten_max[:, :], ident[0:10, 0:10]).then_inc(s_tenr, 1)
                    pe.wait_ge(s_first, 1)
                    pe.matmul(p_c[:, 0:NCH], ones[0:1, :], row[:, 0, :], start=True, stop=True).then_inc(s_firstb, 1)
                    pe.wait_ge(s_shift, 1)
                    pe.matmul(p_d[:, 2 * P:2 * P + 1], ones[0:1, :], small[0:1, 9:10], start=True,
                              stop=True).then_inc(s_shiftb, 1)

                @block.vector
                def _(dve):
                    done = [0]

                    def link(ins):
                        done[0] += 1
                        ins.then_inc(s_chain, 1)
                        dve.wait_ge(s_chain, done[0])

                    dve.memset(eps[:, :], LN_EPS).then_inc(s_eps, 1)
                    dve.memset(windows[:, 0:1], 0)
                    dve.memset(run_max[:, :, :], -3.0e38)
                    dve.memset(tab_max[:, :, :], 0.0)
                    dve.wait_ge(s_ws, 1)
                    for d in range(2):
                        last = dve.tensor_copy(w_all[:, :, d * COLS + HD:(d + 1) * COLS],
                                               p_a[:, 2 * d * HEADS:2 * (d + 1) * HEADS]
                                               .rearrange("p (c h) -> p c h", c=KC))
                    last.then_inc(s_wsc, 1)
                    link(dve.memset(stats[:, :, :], 0.0))
                    base = done[0]

                    def step(i):
                        n = base + 2 * i
                        dve.wait_ge(s_x, 16 * (i + 1))
                        for u in range(U):
                            last = dve.bn_stats(stats[:, u, :], token_rows[:, ds(i * U + u, 1), 0:D]
                                                .rearrange("p a d -> p (a d)"))
                        last.then_inc(s_chain, 1)
                        dve.wait_ge(s_chain, n + 1)
                        settle(dve, turns)
                        for u in range(U):
                            last = dve.bn_aggr(mv[:, u, :], stats[:, u, :])
                        last.then_inc(s_mv, 1)
                        dve.wait_ge(s_rstd, i + 1)
                        dve.reciprocal(rstd[:, :], rstd[:, :]).then_inc(s_chain, 1)
                        dve.wait_ge(s_chain, n + 2)
                        for u in range(U):
                            after(dve, s_xt, (i - 1) * U + u + 1)
                            dve.tensor_scalar(xn[:, u, :], token_rows[:, ds(i * U + u, 1), 0:D]
                                              .rearrange("p a d -> p (a d)"),
                                              mv[:, u, 0:1], rstd[:, u:u + 1], ALU.subtract, ALU.mult)\
                               .then_inc(s_xn, 1)

                    def largest(i):
                        dve.wait_ge(s_tabc, (i + 1) * U)
                        after(dve, s_max, i)
                        scores = tab[:, :, :].rearrange("p u (d c) -> p d c u", d=2)[:, :, HD:COLS, :]
                        dve.tensor_reduce(ten[:, 0:8].rearrange("p (d h) -> p d h", d=2), scores, AX.X, ALU.max,
                                          apply_absolute_value=True).then_inc(s_big, 1)
                        dve.wait_ge(s_big, i + 1)
                        dve.tensor_tensor(tab_max[:, :, :], tab_max[:, :, :],
                                          ten[:, 0:8].rearrange("p (d h) -> p d h", d=2), ALU.max).then_inc(s_max, 1)

                    step(0)
                    with dve.Fori(1, NG) as i:
                        step(i)
                        largest(i - 1)
                    largest(NG - 1)
                    done[0] = base + 2 * NG

                    dve.wait_ge(s_edge, 32)
                    link(dve.tensor_copy(dst_rel[:, :], dst_i[:, :]))
                    by_chunk = dst_rel[:, :].rearrange("p (c k) -> p c k", k=K)
                    dve.tensor_reduce(lohi[:, 0, :], by_chunk, AX.X, ALU.min).then_inc(s_lohi, 1)
                    dve.tensor_reduce(lohi[:, 1, :], by_chunk, AX.X, ALU.max).then_inc(s_lohi, 1)
                    dve.wait_ge(s_max, NG)
                    dve.tensor_copy(ten[:, 0:8], tab_max[:, :, :].rearrange("p d h -> p (d h)")).then_inc(s_ten, 1)
                    for d in range(2):
                        dve.tensor_reduce(ten[:, 8 + d:9 + d], attr_all[:, d, :], AX.X, ALU.max,
                                          apply_absolute_value=True).then_inc(s_ten, 1)
                    dve.wait_ge(s_lohit, 1)
                    parts = p_a[0:NCB, :].rearrange("p (m b q) -> p m b q", m=2, b=2)
                    dve.tensor_reduce(lohi_c[0:NCB, 0:2], parts[:, 0], AX.X, ALU.min).then_inc(s_lohic, 1)
                    dve.tensor_reduce(lohi_c[0:NCB, 2:4], parts[:, 1], AX.X, ALU.max).then_inc(s_lohic, 1)
                    dve.wait_ge(s_tent, 1)
                    dve.tensor_reduce(ten_max[:, :], p_d[0:10, 0:P], AX.X, ALU.max).then_inc(s_tenc, 1)
                    dve.wait_ge(s_rows, 1)
                    dve.tensor_copy(row[:, 0:2, :], p_b[0:1, 0:2 * NCH].rearrange("p (m c) -> p m c", m=2))\
                       .then_inc(s_first, 1)
                    dve.wait_ge(s_first, 1)
                    link(dve.tensor_tensor(row[:, 1, :], row[:, 1, :], row[:, 0, :], ALU.subtract))
                    link(dve.tensor_copy(span[:, :], row[:, 1, :]))
                    link(dve.tensor_single_scalar(span[:, :], span[:, :], WSH, ALU.logical_shift_right))
                    link(dve.tensor_copy(row[:, 2, :], span[:, :]))
                    link(dve.memset(row[:, 1, :], 1.0))
                    link(dve.tensor_tensor_scan(row[:, 3, :], row[:, 1, :], row[:, 2, :], 0.0, ALU.mult, ALU.add))
                    link(dve.tensor_tensor(row[:, 3, :], row[:, 3, :], row[:, 2, :], ALU.subtract))
                    dve.tensor_copy(before[:, :], row[:, 3, :])
                    link(dve.scalar_tensor_tensor(out=row[:, 1, :], in0=row[:, 2, :], scalar=float(EXTRA),
                                                  in1=row[:, 0, :], op0=ALU.mult, op1=ALU.add))
                    dve.tensor_copy(windows[:, 1:1 + NCH], row[:, 1, :])
                    dve.wait_ge(s_firstb, 1)
                    dve.tensor_tensor(by_chunk, by_chunk, p_c[:, 0:NCH].unsqueeze(2).broadcast_to([P, NCH, K]),
                                      ALU.subtract)
                    dve.wait_ge(s_tenr, 1)
                    link(dve.tensor_copy(small[:, 10:16], p_d[0:1, P + 4:P + 10]))
                    link(dve.tensor_scalar(small[:, 0:4], p_d[0:1, P:P + 4], small[:, 14:15], None, ALU.mult))
                    link(dve.scalar_tensor_tensor(out=small[:, 4:8], in0=small[:, 10:14], scalar=small[:, 15:16],
                                                  in1=small[:, 0:4], op0=ALU.mult, op1=ALU.add))
                    link(dve.tensor_reduce(small[:, 8:9], small[:, 4:8], AX.X, ALU.max))
                    dve.tensor_scalar(small[:, 9:10], small[:, 8:9], -1.0, HEADROOM, ALU.mult, ALU.add)\
                       .then_inc(s_shift, 1)
                    dve.wait_ge(s_shiftb, 1)
                    dve.tensor_copy(neg_shift[:, :], p_d[:, 2 * P:2 * P + 1])

        with ExitStack() as ctx:
            sb, ps, sem = tensors(ctx)
            index = sb("index", [P, RING, K], I32)
            rows = sb("rows", [P, RING, K, ROW])
            part = sb("part", [P, 2, K, COLS])
            msg = sb("msg", [P, 2, K, COLS])
            score = sb("score", [P, 2, K, HEADS])
            ex = sb("ex", [P, 2, K, HEADS])
            val = sb("val", [P, 2, K, HEADS * HD])
            hot = sb("hot", [P, 2, K, W])
            hot_x = sb("hot_x", [P, K, W])
            iota_x = sb("iota_x", [P, W])
            p_win = ps("p_win", [P, 2, 512])
            p_x = ps("p_x", [P, 512])

            turns = sem("pool_turns")
            index_ready = [sem(f"index_ready{s}") for s in range(RING)]
            gathered = [sem(f"gathered{s}") for s in range(RING)]
            rows_used = sem("rows_used")
            parts_ready = sem("parts_ready")
            hot_ready = sem("hot_ready")
            max_taken = sem("max_taken")
            score_ready = sem("score_ready")
            exp_ready = sem("exp_ready")
            val_ready = sem("val_ready")
            summed = sem("window_summed")
            added = sem("window_added")
            x_hot = sem("extra_hot_ready")
            x_summed = sem("extra_window_summed")

            filled = sem("dispatch_filled")
            FILL = 3
            FILLS = NJ // FILL
            assert FILLS * FILL == NJ and FILLS < NIT

            def chunks(eng, begin, step, end=NIT):
                loaded = begin(0)
                for s in range(RING):
                    step(s, s, 0, loaded)
                with eng.Fori(1, end) as it:
                    loaded = begin(it)
                    for s in range(RING):
                        step(it * RING + s, s, it, loaded)

            def load(eng, ap, most):
                return nc.values_load_multi_w_load_instructions(
                    ap, engines=[eng.engine], min_val=0, max_val=most)[1]

            def sum_window(pe, psum, v, one_hot):
                for b in range(2):
                    for k in range(K):
                        pe.matmul(psum[:, b * W:(b + 1) * W], val[:, v, k, b * P:(b + 1) * P], one_hot[:, k, :],
                                  start=(k == 0), stop=(k == K - 1))
                for k in range(K):
                    last = pe.matmul(psum[0:HEADS, 2 * W:3 * W], ex[:, v, k, :], one_hot[:, k, :],
                                     start=(k == 0), stop=(k == K - 1))
                return last

            with nc.Block() as block:
                @block.sync
                def _(sp):
                    def step(c, s, it, _):
                        after(sp, gathered[s], 16 * K * it)
                        sp.dma_start(index[:, s, :], src[c] if isinstance(c, int)
                                     else src[ds(c, 1)].rearrange("a p k -> (a p) k")).then_inc(index_ready[s], 16)

                    pad_view = dispatched.rearrange("(n j p) d -> n p j d", j=FILL, p=P)

                    def fill(it):
                        sp.dma_start(pad_view[it] if isinstance(it, int) else
                                     pad_view[ds(it, 1)].rearrange("n p j d -> (n p) j d"),
                                     pad_row[:, :].unsqueeze(1).broadcast_to([P, FILL, XROW])).then_inc(filled, 16)
                    chunks(sp, fill, step, FILLS)
                    with sp.Fori(FILLS, NIT) as it:
                        for s in range(RING):
                            step(it * RING + s, s, it, None)
                    sp.wait_ge(filled, 16 * FILLS)

                @block.gpsimd
                def _(pool):
                    def step(c, s, it, _):
                        pool.wait_ge(index_ready[s], 16 * (it + 1))
                        after(pool, rows_used, c - RING + 1)
                        settle(pool, turns)
                        for k in range(K):
                            pool.indirect_dma_start(
                                out=rows[:, s, k, :], out_offset=None, in_=table,
                                in_offset=bass.IndirectOffsetOnAxis(ap=index[:, s, k:k + 1], axis=0))\
                                .then_inc(gathered[s], 16)
                    chunks(pool, lambda it: None, step)

                @block.scalar
                def _(act):
                    def step(c, s, it, _):
                        v = s % 2
                        act.wait_ge(score_ready, c + 1)
                        after(act, summed, c - 1)
                        act.activation(ex[:, v, :, :], score[:, v, :, :], ACT.Exp, bias=neg_shift[:, 0:1])\
                           .then_inc(exp_ready, 1)
                    chunks(act, lambda it: None, step)

                @block.tensor
                def _(pe):
                    def begin(it):
                        return load(pe, windows[:, ds(it * RING + 1, RING)], EXTRA * (MAXWIN + 1))

                    def step(c, s, it, loaded):
                        v = s % 2
                        pe.wait_ge(hot_ready, c + 1)
                        pe.wait_ge(val_ready, c + 1)
                        after(pe, added, c - 1)
                        sum_window(pe, p_win[:, v, :], v, hot[:, v, :, :]).then_inc(summed, 1)
                        with pe.If(loaded[s] > EXTRA - 1):
                            ahead, = load(pe, before[:, ds(c, 1)], NCH * MAXWIN)
                            with pe.Fori(0, loaded[s] >> 13) as j:
                                pe.wait_ge(x_hot, ahead + j + 1)
                                sum_window(pe, p_x[:, :], v, hot_x[:, :, :]).then_inc(x_summed, 1)
                            pe.nop()
                    chunks(pe, begin, step)

                @block.vector
                def _(dve):
                    def begin(it):
                        return load(dve, windows[:, ds(it * RING, RING + 1)], EXTRA * (MAXWIN + 1))

                    def first_of(word):
                        return nc.s_assert_within(word & (EXTRA - 1), 0, NP - 1)

                    def add_window(psum, node):
                        for a, b in ((acc[:, :, ds(node, W)], psum[:, 0:2 * W].rearrange("p (b w) -> p b w", b=2)),
                                     (acc_e[:, ds(node, W)], psum[0:HEADS, 2 * W:3 * W])):
                            last = dve.tensor_tensor(a, a, b, ALU.add)
                        return last

                    def step(c, s, it, loaded):
                        v = s % 2
                        per_edge = attr_all[:, :, ds(c * K, K)]
                        dve.wait_ge(gathered[s], 16 * K * (it + 1))
                        for d in range(2):
                            last = dve.tensor_tensor(part[:, d, :, :], rows[:, s, :, d * COLS:(d + 1) * COLS],
                                                     per_edge[:, d, :].unsqueeze(2).broadcast_to([P, K, COLS]), ALU.mult)
                        last.then_inc(parts_ready, 1)
                        after(dve, summed, c - 1)
                        dve.wait_ge(parts_ready, c + 1)
                        dve.tensor_tensor(msg[:, v, :, :], part[:, 0, :, :], part[:, 1, :, :], ALU.add)\
                           .then_inc(rows_used, 1)
                        dve.wait_ge(rows_used, c + 1)
                        raw = msg[:, v, :, HD:COLS]
                        dve.scalar_tensor_tensor(out=score[:, v, :, :], in0=raw, scalar=0.2, in1=raw, op0=ALU.mult,
                                                 op1=ALU.max).then_inc(score_ready, 1)
                        dve.tensor_tensor(hot[:, v, :, :],
                                          dst_rel[:, ds(c * K, K)].unsqueeze(2).broadcast_to([P, K, W]),
                                          iota_w[:, :].unsqueeze(1).broadcast_to([P, K, W]), ALU.is_equal)\
                           .then_inc(hot_ready, 1)
                        dve.wait_ge(score_ready, c + 1)
                        after(dve, max_taken, c)
                        dve.tensor_tensor(run_max[:, :, :], run_max[:, :, :], score[:, v, :, :], ALU.max)\
                           .then_inc(max_taken, 1)
                        dve.wait_ge(exp_ready, c + 1)
                        dve.tensor_tensor(
                            val[:, v, :, :].rearrange("p k (h f) -> p k h f", h=HEADS),
                            msg[:, v, :, 0:HD].unsqueeze(2).broadcast_to([P, K, HEADS, HD]),
                            ex[:, v, :, :].unsqueeze(3).broadcast_to([P, K, HEADS, HD]), ALU.mult)\
                           .then_inc(val_ready, 1)
                        if not isinstance(c, int) or c > 0:
                            finish(c - 1, (s - 1) % RING, loaded[s])
                        extra_windows(c, s, loaded[s + 1])

                    def finish(c, s, word):
                        dve.wait_ge(summed, c + 1)
                        after(dve, added, c)
                        add_window(p_win[:, s % 2, :], first_of(word)).then_inc(added, 1)

                    def extra_windows(c, s, word):
                        with dve.If(word > EXTRA - 1):
                            ahead, = load(dve, before[:, ds(c, 1)], NCH * MAXWIN)
                            dve.tensor_copy(iota_x[:, :], iota_w[:, :])
                            dve.drain()
                            with dve.Fori(0, word >> 13) as j:
                                dve.tensor_scalar(iota_x[:, :], iota_x[:, :], float(W), None, ALU.add)
                                dve.drain()
                                dve.tensor_tensor(hot_x[:, :, :],
                                                  dst_rel[:, ds(c * K, K)].unsqueeze(2).broadcast_to([P, K, W]),
                                                  iota_x[:, :].unsqueeze(1).broadcast_to([P, K, W]), ALU.is_equal)\
                                   .then_inc(x_hot, 1)
                                dve.wait_ge(x_summed, ahead + j + 1)
                                node = nc.s_assert_within(first_of(word) + j * W + W, 0, NP - 1)
                                add_window(p_x[:, :], node)
                                dve.drain()
                            dve.nop()
                    chunks(dve, begin, step)
                    final, = load(dve, windows[:, NCH:NCH + 1], EXTRA * (MAXWIN + 1))
                    finish(NCH - 1, RING - 1, final)


def stage_nodes(nc, tensors, g):
    token_rows, top_w, slot_of, expert_of_tile, expert_f, residual = (
        g[n] for n in ("token_rows", "top_w", "slot_of", "expert_of_tile", "expert_f", "residual"))
    ident, ones, eps, acc, acc_e, run_max, neg_shift = (
        g[n] for n in ("ident", "ones", "eps", "acc", "acc_e", "run_max", "neg_shift"))
    with ExitStack() as nodes:
        nsb, _, _ = tensors(nodes)
        top_v = nsb("top_v", [P, NT, 2])
        top_i = nsb("top_i", [P, NT, 2])

        with ExitStack() as ctx:
            sb, ps, sem = tensors(ctx)
            gate_w = sb("gate_w", [P, KC, E])
            gate_b = sb("gate_b", [P, E])
            beta = sb("beta", [P, D])
            head_max = sb("head_max", [P, HEADS])
            top4 = sb("top4", [HEADS, 1])
            eps4 = sb("eps4", [HEADS, 1])
            diag4 = sb("diag4", [HEADS, HEADS])
            eps_b = sb("eps_b", [P, HEADS])
            inv = sb("inv", [P, NT, HEADS])
            staged = sb("staged", [P, U, 2, P])
            attn = sb("attn", [P, U, D])
            x1 = sb("x1", [P, U, D])
            x1_beta = sb("x1_beta", [P, U, D])
            stats = sb("stats3", [P, U, 6])
            mv = sb("mv3", [P, U, 2])
            rstd = sb("rstd3", [P, U])
            nmr = sb("nmr3", [P, U])
            xn = sb("xn3", [P, U, D])
            xt = sb("xt3", [P, 2, KC, P])
            logits = sb("logits", [P, U, E])
            best = sb("best", [P, U, 8])
            best_i = sb("best_i", [P, U, 8], U32)

            p_g = ps("p_g", [P, 2, 512])
            p_t = ps("p_t", [P, 2, 512])
            p_l = ps("p_l", [P, 512])
            p_e = ps("p_e", [P, 512])
            p_s = ps("p_s", [P, 512])

            s_in = sem("router_loaded")
            s_hm = sem("head_max_ready")
            s_hmt = sem("head_max_transposed")
            s_top = sem("score_max_ready")
            s_eps = sem("eps_scaled")
            s_diag = sem("eps_diagonal")
            s_epsb = sem("eps_broadcast")
            s_et = sem("exp_sums_transposed")
            s_chain = sem("dve_steps3")
            s_inv = sem("inverse_sums")
            s_st = sem("staged")
            s_gt = sem("sums_transposed")
            s_attn = sem("attention_ready")
            s_x1 = sem("residual_added")
            s_xb = sem("beta_added")
            s_bn = sem("stats_ready3")
            s_mv = sem("mean_var_ready3")
            s_sd = sem("deviation_ready3")
            s_rc = sem("rstd_ready3")
            s_nm = sem("normalised3")
            s_xt = sem("rows_transposed3")
            s_xc = sem("rows_t_copied3")
            s_l = sem("logits_summed")
            s_lg = sem("logits_ready")
            s_best = sem("best_ready")
            s_besti = sem("best_index_ready")
            s_top2 = sem("best_kept")
            s_out = sem("residual_stored")
            s_kept = sem("rows_kept3")
            turns = sem("dve_turns3")

            with nc.Block() as block:
                @block.sync
                def _(sp):
                    sp.dma_start(gate_w[:, :, :], g["gate_w"].rearrange("(c p) e -> p c e", p=P)).then_inc(s_in, 16)
                    sp.dma_start(gate_b[:, :], g["gate_b"].partition_broadcast(P)).then_inc(s_in, 16)
                    sp.dma_start(beta[:, :], g["beta"].partition_broadcast(P)).then_inc(s_in, 16)
                    rv = residual.rearrange("(g u p) d -> g p u d", p=P, u=U)

                    def store(i):
                        sp.wait_ge(s_xb, (i + 1) * U)
                        sp.dma_start(rv[i] if isinstance(i, int) else
                                     rv[ds(i, 1)].rearrange("g p u d -> (g p) u d"), x1_beta[:, :, :])\
                          .then_inc(s_out, 16)
                        sp.wait_ge(s_nm, (i + 1) * U)
                        sp.dma_start(token_rows[:, ds(i * U, U), 0:D], xn[:, :, :]).then_inc(s_kept, 16)
                    groups(sp, store)
                    sp.wait_ge(s_out, 16 * NG)
                    sp.wait_ge(s_kept, 16 * NG)

                @block.gpsimd
                def _(pool):
                    pool.wait_ge(s_in, 48)

                    def step(i):
                        for u in range(U):
                            pool.wait_ge(s_attn, i * U + u + 1)
                            after(pool, s_nm, (i - 1) * U + u + 1)
                            after(pool, s_xb, (i - 1) * U + u + 1)
                            pool.tensor_tensor(x1[:, u, :], attn[:, u, :], tile_row(token_rows, i * U + u), ALU.add)\
                                .then_inc(s_x1, 1)
                        after(pool, s_out, 16 * i)
                        for u in range(U):
                            pool.wait_ge(s_x1, i * U + u + 1)
                            pool.tensor_tensor(x1_beta[:, u, :], x1[:, u, :], beta[:, :], ALU.add)\
                                .then_inc(s_xb, 1)
                    groups(pool, step)

                @block.scalar
                def _(act):
                    act.wait_ge(s_top, 1)
                    act.activation(eps4[:, :], top4[:, :], ACT.Exp, bias=neg_shift[0:HEADS, 0:1]).then_inc(s_eps, 1)

                    def stage(i):
                        for u in range(U):
                            t = i * U + u
                            after(act, s_gt, t - U + 1)
                            act.activation(staged[:, u, :, :], acc[:, :, ds(t * P, P)], ACT.Copy).then_inc(s_st, 1)

                    def step(i, more=True):
                        act.wait_ge(s_mv, i + 1)
                        act.activation(rstd[:, :], mv[:, :, 1], ACT.Sqrt, bias=eps[:, 0:1]).then_inc(s_sd, 1)
                        if more:
                            stage(i + 1)
                        act.wait_ge(s_rc, 2 * i + 2)
                        after(act, s_kept, 16 * i)
                        for u in range(U):
                            act.activation(xn[:, u, :], x1[:, u, :], ACT.Identity,
                                           bias=nmr[:, u:u + 1], scale=rstd[:, u:u + 1]).then_inc(s_nm, 1)
                        for u in range(U):
                            t = i * U + u
                            act.wait_ge(s_xt, t + 1)
                            after(act, s_l, t - reuse(u, 2, U) + 1)
                            act.activation(xt[:, u % 2, :, :],
                                           p_t[:, u % 2, 0:D].rearrange("p (c n) -> p c n", c=KC), ACT.Copy)\
                               .then_inc(s_xc, 1)
                    stage(0)
                    step(0)
                    with act.Fori(1, NG - 1) as i:
                        step(i)
                    step(NG - 1, more=False)

                @block.tensor
                def _(pe):
                    pe.wait_ge(s_hm, 1)
                    pe.transpose(p_s[0:HEADS, 0:P], head_max[:, :], ident[:, :]).then_inc(s_hmt, 1)
                    for t in range(NT):
                        last = pe.transpose(p_e[:, t * HEADS:(t + 1) * HEADS], acc_e[:, t * P:(t + 1) * P],
                                            ident[0:HEADS, 0:HEADS])
                    last.then_inc(s_et, 1)
                    pe.wait_ge(s_diag, 1)
                    pe.matmul(p_s[:, P:P + HEADS], ones[0:HEADS, :], diag4[:, :], start=True, stop=True)\
                      .then_inc(s_epsb, 1)
                    pe.wait_ge(s_in, 48)

                    def sums(i):
                        for u in range(U):
                            t = i * U + u
                            pe.wait_ge(s_st, t + 1)
                            after(pe, s_attn, t - reuse(u, 2, U) + 1)
                            for b in range(2):
                                last = pe.transpose(p_g[:, u % 2, b * P:(b + 1) * P], staged[:, u, b, :],
                                                    ident[:, :])
                            last.then_inc(s_gt, 1)

                    def product(i, u):
                        t = i * U + u
                        pe.wait_ge(s_xc, t + 1)
                        for c in range(KC):
                            last = pe.matmul(p_l[:, u * E:(u + 1) * E], xt[:, u % 2, c, :], gate_w[:, c, :],
                                             start=(c == 0), stop=(c == KC - 1))
                        last.then_inc(s_l, 1)

                    def step(i, more=True):
                        if more:
                            sums(i + 1)
                        after(pe, s_lg, i)
                        for u in range(U):
                            t = i * U + u
                            pe.wait_ge(s_nm, t + 1)
                            after(pe, s_xc, t - reuse(u, 2, U) + 1)
                            for c in range(KC):
                                last = pe.transpose(p_t[:, u % 2, c * P:(c + 1) * P],
                                                    xn[:, u, c * P:(c + 1) * P], ident[:, :])
                            last.then_inc(s_xt, 1)
                            if u:
                                product(i, u - 1)
                        product(i, U - 1)
                    sums(0)
                    step(0)
                    with pe.Fori(1, NG - 1) as i:
                        step(i)
                    step(NG - 1, more=False)

                @block.vector
                def _(dve):
                    dve.tensor_reduce(head_max[:, :], run_max[:, :, :].rearrange("p k h -> p h k"), AX.X, ALU.max)\
                       .then_inc(s_hm, 1)
                    dve.wait_ge(s_hmt, 1)
                    dve.tensor_reduce(top4[:, :], p_s[0:HEADS, 0:P], AX.X, ALU.max).then_inc(s_top, 1)
                    dve.wait_ge(s_eps, 1)
                    dve.tensor_scalar(diag4[:, :], ident[0:HEADS, 0:HEADS], eps4[:, 0:1], 1e-10, ALU.mult, ALU.mult)\
                       .then_inc(s_diag, 1)
                    dve.wait_ge(s_epsb, 1)
                    dve.tensor_copy(eps_b[:, :], p_s[:, P:P + HEADS]).then_inc(s_chain, 1)
                    dve.wait_ge(s_chain, 1)
                    dve.wait_ge(s_et, 1)
                    dve.tensor_tensor(inv[:, :, :], p_e[:, 0:NT * HEADS].rearrange("p (t h) -> p t h", h=HEADS),
                                      eps_b[:, :].unsqueeze(1).broadcast_to([P, NT, HEADS]), ALU.add)\
                       .then_inc(s_chain, 1)
                    dve.wait_ge(s_chain, 2)
                    dve.reciprocal(inv[:, :, :], inv[:, :, :]).then_inc(s_chain, 1)
                    dve.wait_ge(s_chain, 3)
                    dve.wait_ge(s_in, 48)

                    def attention(i):
                        for u in range(U):
                            t = i * U + u
                            dve.wait_ge(s_gt, t + 1)
                            after(dve, s_x1, t - U + 1)
                            dve.tensor_tensor(attn[:, u, :].rearrange("p (h f) -> p h f", h=HEADS),
                                              p_g[:, u % 2, 0:D].rearrange("p (h f) -> p h f", h=HEADS),
                                              inv[:, ds(t, 1), :].rearrange("p a h -> p (a h)").unsqueeze(2)
                                              .broadcast_to([P, HEADS, HD]), ALU.mult).then_inc(s_attn, 1)

                    def step(i, more=True):
                        for u in range(U):
                            dve.wait_ge(s_x1, i * U + u + 1)
                            last = dve.bn_stats(stats[:, u, :], x1[:, u, :])
                        last.then_inc(s_bn, 1)
                        dve.wait_ge(s_bn, i + 1)
                        after(dve, s_nm, i * U)
                        settle(dve, turns)
                        for u in range(U):
                            last = dve.bn_aggr(mv[:, u, :], stats[:, u, :])
                        last.then_inc(s_mv, 1)
                        dve.wait_ge(s_sd, i + 1)
                        dve.reciprocal(rstd[:, :], rstd[:, :]).then_inc(s_rc, 1)
                        dve.wait_ge(s_rc, 2 * i + 1)
                        dve.scalar_tensor_tensor(out=nmr[:, :], in0=mv[:, :, 0], scalar=-1.0, in1=rstd[:, :],
                                                 op0=ALU.mult, op1=ALU.mult).then_inc(s_rc, 1)
                        if more:
                            attention(i + 1)
                        dve.wait_ge(s_l, (i + 1) * U)
                        dve.tensor_tensor(logits[:, :, :], p_l[:, 0:U * E].rearrange("p (u e) -> p u e", e=E),
                                          gate_b[:, :].unsqueeze(1).broadcast_to([P, U, E]), ALU.add)\
                           .then_inc(s_lg, 1)
                        dve.wait_ge(s_lg, i + 1)
                        settle(dve, turns)
                        for u in range(U):
                            last = dve.max(best[:, u, :], logits[:, u, :])
                        last.then_inc(s_best, 1)
                        dve.wait_ge(s_best, i + 1)
                        settle(dve, turns)
                        for u in range(U):
                            last = dve.max_index(best_i[:, u, :], best[:, u, :], logits[:, u, :])
                        last.then_inc(s_besti, 1)
                        dve.wait_ge(s_besti, i + 1)
                        dve.tensor_copy(top_v[:, ds(i * U, U), :], best[:, :, 0:2])
                        dve.tensor_copy(top_i[:, ds(i * U, U), :], best_i[:, :, 0:2]).then_inc(s_top2, 1)
                        dve.wait_ge(s_top2, i + 1)
                    attention(0)
                    step(0)
                    with dve.Fori(1, NG - 1) as i:
                        step(i)
                    step(NG - 1, more=False)

        with ExitStack() as ctx:
            sb, ps, sem = tensors(ctx)
            earlier = sb("earlier", [P, P], BF16)
            ones_b = sb("ones_b", [P, P], BF16)
            iota_e = sb("iota_e", [P, E])
            iota_m = sb("iota_m", [P, NT])
            iota_j = sb("iota_j", [P, NJ])
            pad_add = sb("pad_add", [P, 1])
            takes = sb("takes", [P, E, G2], BF16)
            total = sb("total", [P, E, G2])
            carry = sb("carry", [P, E, G2])
            reset = sb("reset", [P, E, G2])
            many = sb("many", [P, E, NT])
            ntile = sb("ntile", [P, E])
            ends = sb("ends", [P, E])
            first_slot = sb("first_slot", [P, E])
            cmp = sb("cmp", [P, NJ, E])
            slot_f = sb("slot_f", [P, G2])
            gap = sb("gap", [P, NT])
            p_pre = ps("p_pre", [P, 4, 512])
            p_tot = ps("p_tot", [P, 4, 512])
            s_c = sem("constants4")
            s_c2 = sem("constants4_chain")
            s_take = sem("takes_ready")
            s_pre = sem("counts_summed")
            s_tot = sem("totals_copied")
            s_chain = sem("dve_steps4")
            s_gap = sem("logit_gap")
            s_exp = sem("second_exp")
            QE = E // 4
            with nc.Block() as block:
                @block.gpsimd
                def _(pool):
                    pool.memset(earlier[:, :], 1.0).then_inc(s_c2, 1)
                    pool.memset(pad_add[:, :], float(E)).then_inc(s_c2, 1)
                    pool.memset(reset[:, :, :], 1.0).then_inc(s_c2, 1)
                    pool.wait_ge(s_c2, 3)
                    pool.affine_select(out=earlier[:, :], in_=earlier[:, :], compare_op=ALU.is_gt, fill=0.0,
                                       base=0, pattern=[[1, P]], channel_multiplier=-1).then_inc(s_c, 1)
                    pool.affine_select(out=pad_add[:, :], in_=pad_add[:, :], compare_op=ALU.is_ge, fill=0.0,
                                       base=-LAST, pattern=[[0, 1]], channel_multiplier=1).then_inc(s_c, 1)
                    pool.memset(reset[:, :, 0:1], 0.0).then_inc(s_c, 1)
                    pool.memset(ones_b[:, :], 1.0).then_inc(s_c, 1)
                    for tile, n, step in ((iota_e, E, 1), (iota_m, NT, P), (iota_j, NJ, 1)):
                        pool.iota(tile[:, :], pattern=[[step, n]], base=0, channel_multiplier=0,
                                  allow_small_or_imprecise_dtypes=True).then_inc(s_c, 1)
                    pool.iota(token_rows[:, :, D], pattern=[[P, NT]], base=0, channel_multiplier=1,
                              allow_small_or_imprecise_dtypes=True).then_inc(s_c, 1)

                @block.scalar
                def _(act):
                    act.wait_ge(s_gap, 1)
                    act.activation(gap[:, :], gap[:, :], ACT.Exp).then_inc(s_exp, 1)
                    act.wait_ge(s_pre, 1)
                    act.activation(total[:, :, :].rearrange("p (q e) g -> p q (e g)", q=4), p_tot[:, :, 0:QE * G2],
                                   ACT.Copy).then_inc(s_tot, 1)

                @block.tensor
                def _(pe):
                    pe.wait_ge(s_take, 1)
                    for q in range(4):
                        rhs = takes[:, q * QE:(q + 1) * QE, :].rearrange("p e g -> p (e g)")
                        pe.matmul(p_pre[:, q, 0:QE * G2], earlier[:, :], rhs, start=True, stop=True)
                        last = pe.matmul(p_tot[:, q, 0:QE * G2], ones_b[:, :], rhs, start=True, stop=True)
                    last.then_inc(s_pre, 1)

                @block.vector
                def _(dve):
                    done = [0]

                    def link(ins):
                        done[0] += 1
                        ins.then_inc(s_chain, 1)
                        dve.wait_ge(s_chain, done[0])

                    dve.wait_ge(s_c, 8)
                    dve.tensor_tensor(gap[:, :], top_v[:, :, 1], top_v[:, :, 0], ALU.subtract).then_inc(s_gap, 1)
                    link(dve.tensor_scalar(top_i[:, NT - 1, :], top_i[:, NT - 1, :], pad_add[:, 0:1], None, ALU.add))
                    flat_i = top_i[:, :, :].rearrange("p t k -> p (t k)")
                    link(dve.tensor_tensor(takes[:, :, :], flat_i.unsqueeze(1).broadcast_to([P, E, G2]),
                                           iota_e[:, :].unsqueeze(2).broadcast_to([P, E, G2]), ALU.is_equal))
                    dve.nop().then_inc(s_take, 1)
                    dve.tensor_copy(token_rows[:, :, D + 1], top_i[:, :, 1])
                    dve.wait_ge(s_exp, 1)
                    link(dve.tensor_scalar(top_w[:, :, 1], gap[:, :], 1.0, None, ALU.add))
                    link(dve.reciprocal(top_w[:, :, 0], top_w[:, :, 1]))
                    link(dve.tensor_tensor(top_w[:, :, 1], gap[:, :], top_w[:, :, 0], ALU.mult))
                    dve.wait_ge(s_tot, 1)
                    flat = "p e g -> p (e g)"
                    link(dve.tensor_tensor_scan(carry[:, :, :].rearrange(flat), reset[:, :, :].rearrange(flat),
                                                total[:, :, :].rearrange(flat), 0.0, ALU.mult, ALU.add))
                    link(dve.tensor_tensor(many[:, :, :], carry[:, :, G2 - 1:G2].broadcast_to([P, E, NT]),
                                           iota_m[:, :].unsqueeze(1).broadcast_to([P, E, NT]), ALU.is_gt))
                    link(dve.tensor_reduce(ntile[:, :], many[:, :, :], AX.X, ALU.add))
                    link(dve.tensor_tensor_scan(ends[:, :], ones[:, 0:E], ntile[:, :], 0.0, ALU.mult, ALU.add))
                    link(dve.tensor_tensor(first_slot[:, :], ends[:, :], ntile[:, :], ALU.subtract))
                    link(dve.tensor_scalar(first_slot[:, :], first_slot[:, :], float(P), None, ALU.mult))
                    link(dve.tensor_tensor(carry[:, :, :], carry[:, :, :], total[:, :, :], ALU.subtract))
                    link(dve.tensor_tensor(carry[:, :, :], carry[:, :, :],
                                           first_slot[:, :].unsqueeze(2).broadcast_to([P, E, G2]), ALU.add))
                    by_bank = carry[:, :, :].rearrange("p (q e) g -> p q (e g)", q=4)
                    link(dve.tensor_tensor(by_bank, by_bank, p_pre[:, :, 0:QE * G2], ALU.add))
                    link(dve.tensor_tensor(carry[:, :, :], carry[:, :, :], takes[:, :, :], ALU.mult))
                    link(dve.tensor_reduce(slot_f[:, :], carry[:, :, :].rearrange("p e g -> p g e"), AX.X, ALU.add))
                    link(dve.tensor_scalar(gap2(slot_of), flat_i, float(E), FAR, ALU.is_ge, ALU.mult))
                    link(dve.tensor_tensor(gap2(slot_of), gap2(slot_of), slot_f[:, :], ALU.add))
                    link(dve.tensor_tensor(cmp[:, :, :], ends[:, :].unsqueeze(1).broadcast_to([P, NJ, E]),
                                           iota_j[:, :].unsqueeze(2).broadcast_to([P, NJ, E]), ALU.is_le))
                    link(dve.tensor_reduce(expert_f[:, :], cmp[:, :, :], AX.X, ALU.add))
                    link(dve.tensor_scalar(expert_f[:, :], expert_f[:, :], float(E - 1), None, ALU.min))
                    dve.tensor_copy(expert_of_tile[:, :], expert_f[0:1, :])


def gap2(slot_of):
    return slot_of[:, :, :].rearrange("p t k -> p (t k)")


def stage_experts(nc, tensors, g):
    token_rows, top_w, slot_of, expert_of_tile, expert_f = (
        g[n] for n in ("token_rows", "top_w", "slot_of", "expert_of_tile", "expert_f"))
    ident, eps, dispatched, expert_rows, residual = (
        g[n] for n in ("ident", "eps", "dispatched", "expert_rows", "residual"))

    with ExitStack() as ctx:
        sb, ps, sem = tensors(ctx)
        w1_sb = sb("w1_sb", [P, E, KC, F])
        w2_sb = sb("w2_sb", [P, E, FC, D])
        b1_sb = sb("b1_sb", [P, E * FC])
        meta = sb("meta", [P, NJ, 2])
        back = sb("back", [P, NJ])
        back_i = sb("back_i", [P, 2, 1], I32)
        xs = sb("xs", [P, 2, D])
        xt = sb("xt5", [P, 2, KC, P])
        hid = sb("hid", [P, 2, F])
        hid_t = sb("hid_t", [P, 2, FC, P])
        b2_t = sb("b2_t", [P, 2, D])
        ys = sb("ys", [P, 2, D])
        p_x = ps("p_x5", [P, 2, 512])
        p_h = ps("p_h", [P, 2, 512])
        p_ht = ps("p_ht", [P, 2, 512])
        p_y = ps("p_y", [P, 2, 512])

        turns = sem("pool_turns5")
        s_w = sem("expert_weights")
        s_sent = sem("rows_dispatched")
        s_meta = sem("meta_loaded")
        s_back = sem("back_ready")
        s_xs = [sem(f"xs_loaded{u}") for u in range(2)]
        s_b2 = [sem(f"b2_loaded{u}") for u in range(2)]
        s_t = sem("xs_transposed")
        s_tc = sem("xt_copied")
        s_h = sem("hidden_summed")
        s_hc = sem("hidden_copied")
        s_ht = sem("hidden_transposed")
        s_r = sem("relu_done")
        s_y = sem("result_summed")
        s_ys = sem("result_ready")
        s_bi = sem("back_index_ready")
        s_gone = [sem(f"result_scattered{u}") for u in range(2)]

        def pairs(eng, step):
            for u in range(2):
                step(u, u, 0, False)
            with eng.Fori(1, NJ // 2 - 1) as i:
                for u in range(2):
                    step(i * 2 + u, u, i, False)
            for u in range(2):
                step(NJ - 2 + u, u, NJ // 2 - 1, True)

        with nc.Block() as block:
            @block.gpsimd
            def _(pool):
                flat = slot_of[:, :, :].rearrange("p t k -> p (t k)")
                for n in range(G2):
                    pool.indirect_dma_start(
                        out=dispatched, out_offset=bass.IndirectOffsetOnAxis(ap=flat[:, n:n + 1], axis=0),
                        in_=token_rows[:, n // 2, :], in_offset=None, bounds_check=SLOTS - 1, oob_is_err=False)\
                        .then_inc(s_sent, 16)

                def step(j, u, i, last):
                    pool.wait_ge(s_bi, j + 1)
                    pool.wait_ge(s_ys, j + 1)
                    settle(pool, turns)
                    pool.indirect_dma_start(
                        out=expert_rows, out_offset=bass.IndirectOffsetOnAxis(ap=back_i[:, u, :], axis=0),
                        in_=ys[:, u, :], in_offset=None, bounds_check=2 * NP - 1, oob_is_err=False)\
                        .then_inc(s_gone[u], 16)
                pairs(pool, step)
                for u in range(2):
                    pool.wait_ge(s_gone[u], 16 * (NJ // 2))

            @block.sync
            def _(sp):
                sp.dma_start(b1_sb[:, :], g["b1"]).then_inc(s_w, 16)
                for e in range(0, E, 4):
                    sp.dma_start(w1_sb[:, e:e + 4, :, :],
                                 g["w1"][e:e + 4].rearrange("e (c p) f -> p e c f", p=P)).then_inc(s_w, 16)
                    sp.dma_start(w2_sb[:, e:e + 4, :, :],
                                 g["w2"][e:e + 4].rearrange("e (c p) d -> p e c d", p=P)).then_inc(s_w, 16)
                sp.wait_ge(s_sent, 16 * G2)
                sp.dma_start(meta[:, :, :], dispatched[:, D:XROW].rearrange("(j p) m -> p j m", p=P))\
                  .then_inc(s_meta, 16)
                rv = dispatched.rearrange("(j p) d -> j p d", p=P)

                def step(j, u, i, last):
                    after(sp, s_t, j - 1)
                    sp.dma_start(xs[:, u, :], rv[j][:, 0:D] if isinstance(j, int) else
                                 rv[ds(j, 1), :, 0:D].rearrange("a p d -> (a p) d")).then_inc(s_xs[u], 16)
                    e = nc.values_load_multi_w_load_instructions(
                        expert_of_tile[:, j:j + 1] if isinstance(j, int) else expert_of_tile[:, ds(j, 1)],
                        engines=[sp.engine], min_val=0, max_val=E - 1)[1][0]
                    after(sp, s_ys, j - 1)
                    sp.dma_start(b2_t[:, u, :], g["b2"][ds(e, 1), :].rearrange("a d -> (a d)")
                                 .partition_broadcast(P)).then_inc(s_b2[u], 16)
                pairs(sp, step)

            @block.scalar
            def _(act):
                def rows_t(j, u):
                    act.wait_ge(s_t, j + 1)
                    after(act, s_h, j - 1)
                    act.activation(xt[:, u, :, :], p_x[:, u, 0:D].rearrange("p (c n) -> p c n", c=KC), ACT.Copy)\
                       .then_inc(s_tc, 1)

                def relu(j, u, e):
                    act.wait_ge(s_ht, j + 1)
                    after(act, s_y, j - 1)
                    for c in range(FC):
                        last = act.activation(hid_t[:, u, c, :], p_ht[:, u, c * P:(c + 1) * P], ACT.Relu,
                                              bias=b1_sb[:, ds(e * FC + c, 1)])
                    last.then_inc(s_r, 1)

                def step(j, u, i, last):
                    if u == 0:
                        self_e[:] = nc.values_load_multi_w_load_instructions(
                            expert_of_tile[:, ds(i * 2, 2)], engines=[act.engine], min_val=0, max_val=E - 1)[1]
                    relu(j, u, self_e[u])
                    if not last:
                        rows_t(j + 2, u)
                self_e = [0, 0]
                rows_t(0, 0)
                rows_t(1, 1)
                act.wait_ge(s_w, 16 * 9)
                pairs(act, step)

            @block.tensor
            def _(pe):
                def rows_t(j, u, i):
                    pe.wait_ge(s_xs[u], 16 * (i + 1))
                    after(pe, s_tc, j - 1)
                    for c in range(KC):
                        last = pe.transpose(p_x[:, u, c * P:(c + 1) * P], xs[:, u, c * P:(c + 1) * P], ident[:, :])
                    last.then_inc(s_t, 1)

                def first_layer(j, u, e):
                    pe.wait_ge(s_tc, j + 1)
                    after(pe, s_hc, j - 1)
                    for c in range(KC):
                        last = pe.matmul(p_h[:, u, :], xt[:, u, c, :], w1_sb[:, ds(e, 1), c, :]
                                         .rearrange("p a f -> p (a f)"), start=(c == 0), stop=(c == KC - 1))
                    last.then_inc(s_h, 1)

                def hidden_t(j, u):
                    pe.wait_ge(s_hc, j + 1)
                    after(pe, s_r, j - 1)
                    for c in range(FC):
                        last = pe.transpose(p_ht[:, u, c * P:(c + 1) * P], hid[:, u, c * P:(c + 1) * P], ident[:, :])
                    last.then_inc(s_ht, 1)

                def second_layer(j, u, e):
                    pe.wait_ge(s_r, j + 1)
                    after(pe, s_ys, j - 1)
                    for c in range(FC):
                        last = pe.matmul(p_y[:, u, 0:D], hid_t[:, u, c, :], w2_sb[:, ds(e, 1), c, :]
                                         .rearrange("p a d -> p (a d)"), start=(c == 0), stop=(c == FC - 1))
                    last.then_inc(s_y, 1)

                def load(i, n):
                    return nc.values_load_multi_w_load_instructions(
                        expert_of_tile[:, ds(i * 2, n)], engines=[pe.engine], min_val=0, max_val=E - 1)[1]

                rows_t(0, 0, 0)
                rows_t(1, 1, 0)
                pe.wait_ge(s_w, 16 * 9)
                first_layer(0, 0, load(0, 1)[0])
                experts = [None]

                def step(j, u, i, last):
                    if u == 0:
                        experts[0] = load(i, 2 if last else 3)
                    hidden_t(j, u)
                    if not (last and u):
                        first_layer(j + 1, 1 - u, experts[0][u + 1])
                    if not last:
                        rows_t(j + 2, u, i + 1)
                    second_layer(j, u, experts[0][u])
                pairs(pe, step)

            @block.vector
            def _(dve):
                dve.wait_ge(s_meta, 16)
                dve.tensor_tensor(back[:, :], meta[:, :, 1], expert_f[:, :], ALU.is_equal).then_inc(s_back, 1)
                dve.wait_ge(s_back, 1)
                dve.scalar_tensor_tensor(out=back[:, :], in0=back[:, :], scalar=float(NP), in1=meta[:, :, 0],
                                         op0=ALU.mult, op1=ALU.add).then_inc(s_back, 1)
                dve.wait_ge(s_back, 2)

                def hidden(j, u):
                    dve.wait_ge(s_h, j + 1)
                    after(dve, s_ht, j - 1)
                    dve.tensor_copy(hid[:, u, :], p_h[:, u, :]).then_inc(s_hc, 1)

                def step(j, u, i, last):
                    if not (last and u):
                        hidden(j + 1, 1 - u)
                    after(dve, s_gone[u], 16 * i)
                    dve.tensor_copy(back_i[:, u, :], back[:, ds(j, 1)]).then_inc(s_bi, 1)
                    dve.wait_ge(s_y, j + 1)
                    dve.wait_ge(s_b2[u], 16 * (i + 1))
                    dve.tensor_tensor(ys[:, u, :], p_y[:, u, 0:D], b2_t[:, u, :], ALU.add).then_inc(s_ys, 1)
                hidden(0, 0)
                pairs(dve, step)

    with ExitStack() as ctx:
        sb, ps, sem = tensors(ctx)
        gamma = sb("gamma", [P, D])
        y0 = sb("y0", [P, U, D])
        y1 = sb("y1", [P, U, D])
        res = sb("res", [P, U, D])
        mix = sb("mix", [P, U, D])
        norm = sb("norm", [P, U, D])
        final = sb("final", [P, U, D])
        stats = sb("stats6", [P, U, 6])
        mv = sb("mv6", [P, U, 2])
        rstd = sb("rstd6", [P, U])
        nmr = sb("nmr6", [P, U])
        turns = sem("dve_turns6")
        s_g = sem("gamma_loaded")
        s_in = [sem(f"expert_rows_loaded{u}") for u in range(U)]
        s_res = [sem(f"residual_loaded{u}") for u in range(U)]
        s_m0 = sem("first_choice_added")
        s_m1 = sem("second_choice_added")
        s_bn = sem("stats_ready6")
        s_mv = sem("mean_var_ready6")
        s_sd = sem("deviation_ready6")
        s_rc = sem("rstd_ready6")
        s_nm = sem("normalised6")
        s_gm = sem("gamma_applied")
        s_f = sem("final_ready")
        s_out = [sem(f"final_stored{u}") for u in range(U)]

        with nc.Block() as block:
            @block.sync
            def _(sp):
                sp.dma_start(gamma[:, :], g["gamma"].partition_broadcast(P)).then_inc(s_g, 16)
                yv = expert_rows.rearrange("(k t p) d -> k t p d", k=2, p=P)
                rv = residual.rearrange("(t p) d -> t p d", p=P)

                def step(i):
                    for u in range(U):
                        t = i * U + u
                        after(sp, s_m1, t - U + 1)
                        tile(y0, yv[0], t, u, s_in[u])
                        tile(y1, yv[1], t, u, s_in[u])
                    for u in range(U):
                        after(sp, s_f, i * U + u - U + 1)
                        tile(res, rv, i * U + u, u, s_res[u])

                def tile(to, of, t, u, loaded):
                    if isinstance(t, int):
                        real = LAST if t == NT - 1 else P
                        sp.dma_start(to[0:real, u, :], of[t][0:real, :]).then_inc(loaded, 16)
                    else:
                        sp.dma_start(to[:, u, :], of[ds(t, 1)].rearrange("a p d -> (a p) d")).then_inc(loaded, 16)
                groups(sp, step)

            @block.scalar
            def _(act):
                ov = out_tiles(g["out"])

                def step(i):
                    act.wait_ge(s_mv, i + 1)
                    act.activation(rstd[:, :], mv[:, :, 1], ACT.Sqrt, bias=eps[:, 0:1]).then_inc(s_sd, 1)
                    act.wait_ge(s_rc, 2 * i + 2)
                    for u in range(U):
                        after(act, s_gm, (i - 1) * U + u + 1)
                        act.activation(norm[:, u, :], mix[:, u, :], ACT.Identity, bias=nmr[:, u:u + 1],
                                       scale=rstd[:, u:u + 1]).then_inc(s_nm, 1)
                    for u in range(U):
                        t = i * U + u
                        act.wait_ge(s_f, t + 1)
                        if isinstance(t, int) and t == NT - 1:
                            act.dma_start(g["out"][t * P:N, :], final[0:LAST, u, :]).then_inc(s_out[u], 16)
                        else:
                            act.dma_start(ov[t] if isinstance(t, int) else ov[ds(t, 1)].rearrange("a p d -> (a p) d"),
                                          final[:, u, :]).then_inc(s_out[u], 16)
                groups(act, step)
                for u in range(U):
                    act.wait_ge(s_out[u], 16 * NG)

            @block.gpsimd
            def _(pool):
                def step(i):
                    for u in range(U):
                        pool.wait_ge(s_gm, i * U + u + 1)
                        pool.wait_ge(s_res[u], 16 * (i + 1))
                        after(pool, s_out[u], 16 * i)
                        pool.tensor_tensor(final[:, u, :], norm[:, u, :], res[:, u, :], ALU.add).then_inc(s_f, 1)
                groups(pool, step)

            @block.vector
            def _(dve):
                dve.wait_ge(s_g, 16)

                def step(i):
                    for u in range(U):
                        t = i * U + u
                        dve.wait_ge(s_in[u], 32 * (i + 1))
                        after(dve, s_nm, (i - 1) * U + u + 1)
                        dve.scalar_tensor_tensor(out=mix[:, u, :], in0=y0[:, u, :], scalar=weight(t, 0),
                                                 in1=tile_row(token_rows, t), op0=ALU.mult, op1=ALU.add)\
                           .then_inc(s_m0, 1)
                    for u in range(U):
                        t = i * U + u
                        dve.wait_ge(s_m0, t + 1)
                        dve.scalar_tensor_tensor(out=mix[:, u, :], in0=y1[:, u, :], scalar=weight(t, 1),
                                                 in1=mix[:, u, :], op0=ALU.mult, op1=ALU.add).then_inc(s_m1, 1)
                    for u in range(U):
                        dve.wait_ge(s_m1, i * U + u + 1)
                        last = dve.bn_stats(stats[:, u, :], mix[:, u, :])
                    last.then_inc(s_bn, 1)
                    dve.wait_ge(s_bn, i + 1)
                    settle(dve, turns)
                    for u in range(U):
                        last = dve.bn_aggr(mv[:, u, :], stats[:, u, :])
                    last.then_inc(s_mv, 1)
                    if not (isinstance(i, int) and i == 0):
                        gamma_mult(i - 1)
                    dve.wait_ge(s_sd, i + 1)
                    dve.reciprocal(rstd[:, :], rstd[:, :]).then_inc(s_rc, 1)
                    dve.wait_ge(s_rc, 2 * i + 1)
                    dve.scalar_tensor_tensor(out=nmr[:, :], in0=mv[:, :, 0], scalar=-1.0, in1=rstd[:, :],
                                             op0=ALU.mult, op1=ALU.mult).then_inc(s_rc, 1)

                def weight(t, k):
                    return top_w[:, t, k:k + 1] if isinstance(t, int) else \
                        top_w[:, ds(t, 1), k:k + 1].rearrange("p a b -> p (a b)")

                def gamma_mult(i):
                    for u in range(U):
                        dve.wait_ge(s_nm, i * U + u + 1)
                        dve.tensor_tensor(norm[:, u, :], norm[:, u, :], gamma[:, :], ALU.mult).then_inc(s_gm, 1)
                groups(dve, step)
                gamma_mult(NG - 1)


def out_tiles(out):
    return out[0:(NT - 1) * P, :].rearrange("(t p) d -> t p d", p=P)


def tile_row(rows, t, at=0, n=D):
    if isinstance(t, int):
        return rows[:, t, at:at + n]
    return rows[:, ds(t, 1), at:at + n].rearrange("p a d -> p (a d)")


def kernel(**inputs):
    import numpy as np
    import concourse.bacc as bacc
    from concourse.bass_utils import run_bass_kernel_spmd

    a = {k: np.asarray(v) for k, v in inputs.items()}
    pad = NCH * CHUNK - EDGES
    src = np.pad(a["src"], (0, pad), mode="edge").reshape(NCH, P, K)
    dst = np.pad(a["dst"], (0, pad), constant_values=NP - 1).reshape(NCH, P, K).transpose(1, 0, 2)
    attr = np.pad(a["edge_attr_2"], ((0, pad), (0, 0)), mode="edge").reshape(NCH, P, K, 2).transpose(1, 3, 0, 2)
    arrays = {
        "x": np.pad(a["x"], ((0, NP - N), (0, 0))),
        "src": src,
        "dst": dst.reshape(P, NCH * K),
        "attr": attr.reshape(P, 2, NCH * K),
        "w_fwd": a["L0_gnn_W_forward"],
        "w_rev": a["L0_gnn_W_reverse"],
        "w_fwd_t": a["L0_gnn_W_forward"].T,
        "w_rev_t": a["L0_gnn_W_reverse"].T,
        "attn_t": a["L0_gnn_attn_forward"][0].T,
        "gate_w": a["L0_ffn_gate_w"],
        "gate_b": a["L0_ffn_gate_b"],
        "w1": a["L0_ffn_w1"],
        "b1": a["L0_ffn_b1"].reshape(E * FC, P).T,
        "w2": a["L0_ffn_w2"],
        "b2": a["L0_ffn_b2"],
        "gamma": a["L0_ffn_gamma"],
        "beta": a["L0_ffn_beta"],
    }
    nc = bacc.Bacc("TRN2", target_bir_lowering=False, num_devices=1)
    given, feeds = {}, {}
    for name, value in arrays.items():
        value = np.ascontiguousarray(value)
        feeds[f"in_{name}"] = value
        given[name] = nc.dram_tensor(f"in_{name}", value.shape, mybir.dt.from_np(value.dtype),
                                     kind="ExternalInput").ap()
    out = nc.dram_tensor("out", (N, D), F32, kind="ExternalOutput").ap()
    build(nc, **given, out=out)
    r = run_bass_kernel_spmd(nc, [feeds], core_ids=[0])
    return r.results[0]["out"]
```

```python
from contextlib import ExitStack

import concourse.bass as bass
from concourse import mybir

F32 = mybir.dt.float32
BF16 = mybir.dt.bfloat16
I32 = mybir.dt.int32
U32 = mybir.dt.uint32
ALU = mybir.AluOpType
ACT = mybir.ActivationFunctionType
AX = mybir.AxisListType
ds = bass.ds

P = 128
N = 6250
D = 256
HD = 64
HEADS = 4
NT = -(-N // P)
NP = NT * P
LAST = N - (NT - 1) * P
U = 7
NG = NT // U
assert NG * U == NT and NG % 2 == 1

EDGES = 200000
K = 8
CHUNK = K * P
RING = 4
EARLY = 2
NCH = -(-EDGES // (CHUNK * RING)) * RING
NIT = NCH // RING
W = 64
WSH = 6
EXTRA = 8192
MAXWIN = NP // W
COLS = HD + HEADS
ROW = 2 * COLS
NCB = NCH // 2
assert NCB <= P

E = 16
F = 512
KC = D // P
FC = F // P
R5 = 4
LEAST = -(-2 * N // P // R5)
assert LEAST >= 3
NJ = (2 * N + E * (P - 1)) // P + 1
NJ += -NJ % R5
CAP = -(-(N + P) // P) * P
SLOTS = E * CAP + P
XROW = D + 2
STEPS = 5
CONSTANTS = 13
FAR = 1.0e6
LN_EPS = 1e-5
HEADROOM = 40.0


def after(eng, sem, count):
    if isinstance(count, int) and count <= 0:
        return
    eng.wait_ge(sem, count)


def settle(eng, turns):
    eng.sem_inc(turns, 1)


def reuse(u, depth, unroll):
    d = 1
    while ((u - d) % unroll) % depth != u % depth:
        d += 1
    return d


def groups(eng, step):
    step(0)
    with eng.Fori(1, NG - 1) as i:
        step(i)
    step(NG - 1)


def alternate(eng, step):
    step(0, 0, 0)
    step(1, 1, 0)
    with eng.Fori(1, NG // 2) as k:
        for v in range(2):
            step(k * 2 + v, v, k)
    step(NG - 1, 0, NG // 2)


def build(nc, x, src, dst, attr, w_fwd, w_rev, w_fwd_t, w_rev_t, attn_t, gate_w, gate_b,
          w1, b1, w2, b2, gamma, beta, out):
    table = nc.dram_tensor("node_table", (NP, ROW), F32).ap()
    dispatched = nc.dram_tensor("dispatched", (SLOTS, XROW), F32).ap()
    expert_rows = nc.dram_tensor("expert_rows", (2 * NP, D), F32).ap()
    residual = nc.dram_tensor("residual", (NP, D), F32).ap()

    with ExitStack() as whole:
        def tensors(ctx):
            def sb(name, shape, dt=F32):
                return ctx.enter_context(nc.sbuf_tensor(name, shape, dt))

            def ps(name, shape, dt=F32):
                return ctx.enter_context(nc.psum_tensor(name, shape, dt))

            def sem(name):
                return ctx.enter_context(nc.semaphore(name))
            return sb, ps, sem

        sb, _, sem = tensors(whole)
        ident = sb("ident", [P, P])
        ones = sb("ones", [P, P])
        eps = sb("eps", [P, 1])
        iota_w = sb("iota_w", [P, W])
        token_rows = sb("token_rows", [P, NT, D])
        top_w = sb("top_w", [P, NT, 2])
        expert_f = sb("expert_f", [P, NJ])
        expert_of_tile = sb("expert_of_tile", [1, NJ], I32)
        row_of_tile = sb("row_of_tile", [1, NJ], I32)
        more_turns = sb("more_turns", [1, 1], I32)
        run_end = sb("run_end", [1, E], I32)
        pad_row = sb("pad_row", [P, XROW])
        sent = [sem("rows_sent0"), sem("rows_sent1")]

        with ExitStack() as graph:
            gsb, _, _ = tensors(graph)
            acc = gsb("acc", [P, 2, NP + W])
            acc_e = gsb("acc_e", [HEADS, NP + W])
            run_max = gsb("run_max", [P, K, HEADS])
            neg_shift = gsb("neg_shift", [P, 1])
            stage_edges(nc, tensors, locals())
            stage_nodes(nc, tensors, locals())
        stage_experts(nc, tensors, locals())


def stage_edges(nc, tensors, g):
    x, src, dst, attr, table, dispatched = (g[n] for n in ("x", "src", "dst", "attr", "table", "dispatched"))
    ident, ones, eps, iota_w, token_rows, acc, acc_e, run_max, neg_shift = (
        g[n] for n in ("ident", "ones", "eps", "iota_w", "token_rows", "acc", "acc_e", "run_max", "neg_shift"))
    with ExitStack() as edges:
        esb, _, esem = tensors(edges)
        attr_all = esb("attr_all", [P, 2, NCH * K])
        dst_rel = esb("dst_rel", [P, NCH * K])
        windows = esb("windows", [1, 1 + NCH], I32)
        before = esb("before", [1, NCH], I32)

        index = esb("index", [P, RING, K], I32)
        rows = esb("rows", [P, RING, K, ROW])
        index_ready = [esem(f"index_ready{s}") for s in range(RING)]
        gathered = [esem(f"gathered{s}") for s in range(RING)]

        def gather(pool, s):
            for k in range(K):
                pool.indirect_dma_start(out=rows[:, s, k, :], out_offset=None, in_=table,
                                        in_offset=bass.IndirectOffsetOnAxis(ap=index[:, s, k:k + 1], axis=0))\
                    .then_inc(gathered[s], 16)

        with ExitStack() as ctx:
            sb, ps, sem = tensors(ctx)
            dst_i = sb("dst_i", [P, NCH * K], I32)
            w_nat = sb("w_nat", [HD, 2, D])
            attn_sb = sb("attn_sb", [HD, HEADS])
            w_all = sb("w_all", [P, KC, ROW])
            stats = sb("stats", [P, U, 6])
            mv = sb("mv", [P, U, 2])
            rstd = sb("rstd", [P, U])
            xn = sb("xn", [P, U, D])
            xn_t = sb("xn_t", [P, 2, KC, P])
            tab = sb("tab", [P, 2, U, ROW])
            tab_max = sb("tab_max", [P, 2, HEADS])
            ten = sb("ten", [P, 10])
            ten_max = sb("ten_max", [10, 1])
            lohi = sb("lohi", [P, 2, NCH])
            lohi_c = sb("lohi_c", [P, 4])
            row = sb("row", [1, 4, NCH])
            span = sb("span", [1, NCH], I32)
            small = sb("small", [1, 16])

            p_xt = ps("p_xt", [P, 2, 512])
            p_tab = ps("p_tab", [P, 2, 512])
            p_a = ps("p_a", [P, 512])
            p_b = ps("p_b", [P, 512])
            p_c = ps("p_c", [P, 512])
            p_d = ps("p_d", [P, 512])

            s_x = sem("x_loaded")
            s_edge = sem("edges_loaded")
            s_w = sem("weights_loaded")
            s_ident = sem("ident_ready")
            s_chain = sem("dve_steps")
            turns = sem("dve_turns")
            s_eps = sem("eps_ready")
            s_mv = sem("mean_var_ready")
            s_rstd = sem("rstd_ready")
            s_xn = sem("xn_ready")
            s_xt = sem("xn_transposed")
            s_xtc = sem("xn_t_copied")
            s_tab = sem("table_tile_done")
            s_tabc = sem("table_tile_copied")
            s_max = sem("table_max_taken")
            s_big = sem("group_max_taken")
            s_stored = [sem("table_stored0"), sem("table_stored1")]
            s_ws = sem("score_weights_done")
            s_wsc = sem("score_weights_copied")
            s_lohi = sem("chunk_ranges")
            s_lohit = sem("chunk_ranges_transposed")
            s_lohic = sem("chunk_columns")
            s_rows = sem("chunk_rows")
            s_first = sem("first_row")
            s_firstb = sem("first_broadcast")
            s_ten = sem("maxima_columns")
            s_tent = sem("maxima_transposed")
            s_tenc = sem("maxima_reduced")
            s_tenr = sem("maxima_row")
            s_shift = sem("shift_value")
            s_shiftb = sem("shift_broadcast")
            s_init = sem("memory_set")

            with nc.Block() as block:
                @block.sync
                def _(sp):
                    for d, (nat, tr) in enumerate(((g["w_fwd"], g["w_fwd_t"]), (g["w_rev"], g["w_rev_t"]))):
                        sp.dma_start(w_nat[:, d, :], nat).then_inc(s_w, 16)
                        sp.dma_start(w_all[:, :, d * COLS:d * COLS + HD],
                                     tr.rearrange("(c p) f -> p c f", p=P)).then_inc(s_w, 16)
                    sp.dma_start(attn_sb[:, :], g["attn_t"]).then_inc(s_w, 16)
                    xv = x.rearrange("(g u p) d -> g p u d", p=P, u=U)
                    for i in range(NG):
                        sp.dma_start(token_rows[:, i * U:(i + 1) * U, 0:D], xv[i]).then_inc(s_x, 16)
                        if i == 0:
                            sp.dma_start(dst_i[:, :], dst).then_inc(s_edge, 16)
                            sp.dma_start(attr_all[:, :, :], attr).then_inc(s_edge, 16)
                        sp.wait_ge(s_x, 16 * (i + 1))
                    for s in range(RING):
                        sp.dma_start(index[:, s, :], src[s]).then_inc(index_ready[s], 16)

                @block.gpsimd
                def _(pool):
                    pool.memset(ident[:, :], 0.0).then_inc(s_init, 1)
                    pool.wait_ge(s_init, 1)
                    pool.affine_select(out=ident[:, :], in_=ident[:, :], compare_op=ALU.not_equal, fill=1.0,
                                       base=0, pattern=[[-1, P]], channel_multiplier=1).then_inc(s_ident, 1)
                    pool.memset(ones[:, :], 1.0).then_inc(s_ident, 1)
                    pool.iota(iota_w[:, :], pattern=[[1, W]], base=0, channel_multiplier=0,
                              allow_small_or_imprecise_dtypes=True).then_inc(s_ident, 1)
                    pool.memset(acc_e[:, :], 0.0)
                    pool.memset(acc[:, :, :], 0.0)
                    for v in range(2):
                        pool.wait_ge(s_stored[v], 16 * ((NG + 1 - v) // 2))
                    for s in range(EARLY):
                        pool.wait_ge(index_ready[s], 16)
                        gather(pool, s)

                @block.scalar
                def _(act):
                    def copy(t, u):
                        act.wait_ge(s_xt, t + 1)
                        after(act, s_tab, t - reuse(u, 2, U) + 1)
                        act.activation(xn_t[:, u % 2, :, :], p_xt[:, u % 2, 0:D].rearrange("p (c n) -> p c n", c=KC),
                                       ACT.Copy).then_inc(s_xtc, 1)

                    def table_copy(t, u, i, v, k):
                        act.wait_ge(s_tab, t + 1)
                        if u == 0:
                            after(act, s_stored[v], k * 16)
                            after(act, s_max, i - 1)
                        act.activation(tab[:, v, u, :], p_tab[:, u % 2, 0:ROW], ACT.Copy).then_inc(s_tabc, 1)

                    act.wait_ge(s_eps, 1)
                    def deviation(i):
                        act.wait_ge(s_mv, i + 1)
                        act.activation(rstd[:, :], mv[:, :, 1], ACT.Sqrt, bias=eps[:, 0:1]).then_inc(s_rstd, 1)

                    tv = table.rearrange("(g u p) c -> g p u c", p=P, u=U)

                    def step(i, v, k):
                        for u in range(U):
                            copy(i * U + u, u)
                            if u:
                                table_copy(i * U + u - 1, u - 1, i, v, k)
                            if u == U - 3 and not (isinstance(i, int) and i == NG - 1):
                                act.wait_ge(s_xn, (i + 1) * U)
                                deviation(i + 1)
                        table_copy(i * U + U - 1, U - 1, i, v, k)
                        act.wait_ge(s_tabc, (i + 1) * U)
                        act.dma_start(tv[i] if isinstance(i, int) else
                                      tv[ds(i, 1)].rearrange("g p u c -> (g p) u c"), tab[:, v, :, :])\
                           .then_inc(s_stored[v], 16)
                    deviation(0)
                    alternate(act, step)

                @block.tensor
                def _(pe):
                    pe.wait_ge(s_w, 5 * 16)
                    for d in range(2):
                        for c in range(KC):
                            last = pe.matmul(p_a[:, (2 * d + c) * HEADS:(2 * d + c + 1) * HEADS],
                                             w_nat[:, d, c * P:(c + 1) * P], attn_sb[:, :], start=True, stop=True)
                    last.then_inc(s_ws, 1)
                    pe.wait_ge(s_ident, 3)

                    def transpose(t, u):
                        pe.wait_ge(s_xn, t + 1)
                        after(pe, s_xtc, t - reuse(u, 2, U) + 1)
                        for c in range(KC):
                            last = pe.transpose(p_xt[:, u % 2, c * P:(c + 1) * P], xn[:, u, c * P:(c + 1) * P],
                                                ident[:, :])
                        last.then_inc(s_xt, 1)

                    def product(t, u):
                        pe.wait_ge(s_xtc, t + 1)
                        if isinstance(t, int) and t == 0:
                            pe.wait_ge(s_wsc, 1)
                        after(pe, s_tabc, t - reuse(u, 2, U) + 1)
                        for c in range(KC):
                            last = pe.matmul(p_tab[:, u % 2, 0:ROW], xn_t[:, u % 2, c, :], w_all[:, c, :],
                                             start=(c == 0), stop=(c == KC - 1))
                        last.then_inc(s_tab, 1)

                    def step(i):
                        for u in range(U):
                            transpose(i * U + u, u)
                            if u:
                                product(i * U + u - 1, u - 1)
                        product(i * U + U - 1, U - 1)
                    groups(pe, step)

                    pe.wait_ge(s_lohi, 2)
                    for q in range(4):
                        last = pe.transpose(p_a[0:NCB, q * P:(q + 1) * P],
                                            lohi[:, q // 2, (q % 2) * NCB:(q % 2 + 1) * NCB], ident[:, :])
                    last.then_inc(s_lohit, 1)
                    pe.wait_ge(s_ten, 3)
                    pe.transpose(p_d[0:10, 0:P], ten[:, :], ident[:, :]).then_inc(s_tent, 1)
                    pe.wait_ge(s_lohic, 2)
                    for q in range(4):
                        last = pe.transpose(p_b[0:1, q * NCB:(q + 1) * NCB], lohi_c[0:NCB, q:q + 1],
                                            ident[0:NCB, 0:NCB])
                    last.then_inc(s_rows, 1)
                    pe.wait_ge(s_tenc, 1)
                    pe.transpose(p_d[0:1, P:P + 10], ten_max[:, :], ident[0:10, 0:10]).then_inc(s_tenr, 1)
                    pe.wait_ge(s_first, 1)
                    pe.matmul(p_c[:, 0:NCH], ones[0:1, :], row[:, 0, :], start=True, stop=True).then_inc(s_firstb, 1)
                    pe.wait_ge(s_shift, 1)
                    pe.matmul(p_d[:, 2 * P:2 * P + 1], ones[0:1, :], small[0:1, 9:10], start=True,
                              stop=True).then_inc(s_shiftb, 1)

                @block.vector
                def _(dve):
                    done = [0]

                    def link(ins):
                        done[0] += 1
                        ins.then_inc(s_chain, 1)
                        dve.wait_ge(s_chain, done[0])

                    dve.memset(eps[:, :], LN_EPS).then_inc(s_eps, 1)
                    dve.memset(windows[:, 0:1], 0)
                    dve.memset(run_max[:, :, :], -3.0e38)
                    dve.memset(tab_max[:, :, :], 0.0)
                    dve.wait_ge(s_ws, 1)
                    for d in range(2):
                        last = dve.tensor_copy(w_all[:, :, d * COLS + HD:(d + 1) * COLS],
                                               p_a[:, 2 * d * HEADS:2 * (d + 1) * HEADS]
                                               .rearrange("p (c h) -> p c h", c=KC))
                    last.then_inc(s_wsc, 1)
                    link(dve.memset(stats[:, :, :], 0.0))
                    base = done[0]

                    def step(i, v, k):
                        n = base + 2 * i
                        dve.wait_ge(s_x, 16 * (i + 1))
                        for u in range(U):
                            last = dve.bn_stats(stats[:, u, :], token_rows[:, ds(i * U + u, 1), 0:D]
                                                .rearrange("p a d -> p (a d)"))
                        last.then_inc(s_chain, 1)
                        dve.wait_ge(s_chain, n + 1)
                        settle(dve, turns)
                        for u in range(U):
                            last = dve.bn_aggr(mv[:, u, :], stats[:, u, :])
                        last.then_inc(s_mv, 1)
                        dve.wait_ge(s_rstd, i + 1)
                        dve.reciprocal(rstd[:, :], rstd[:, :]).then_inc(s_chain, 1)
                        dve.wait_ge(s_chain, n + 2)
                        for u in range(U):
                            after(dve, s_xt, (i - 1) * U + u + 1)
                            dve.tensor_scalar(xn[:, u, :], token_rows[:, ds(i * U + u, 1), 0:D]
                                              .rearrange("p a d -> p (a d)"),
                                              mv[:, u, 0:1], rstd[:, u:u + 1], ALU.subtract, ALU.mult)\
                               .then_inc(s_xn, 1)
                        if not (isinstance(i, int) and i == 0):
                            largest(i - 1, 1 - v)

                    def largest(i, v):
                        dve.wait_ge(s_tabc, (i + 1) * U)
                        after(dve, s_max, i)
                        scores = tab[:, v, :, :].rearrange("p u (d c) -> p d c u", d=2)[:, :, HD:COLS, :]
                        dve.tensor_reduce(ten[:, 0:8].rearrange("p (d h) -> p d h", d=2), scores, AX.X, ALU.max,
                                          apply_absolute_value=True).then_inc(s_big, 1)
                        dve.wait_ge(s_big, i + 1)
                        dve.tensor_tensor(tab_max[:, :, :], tab_max[:, :, :],
                                          ten[:, 0:8].rearrange("p (d h) -> p d h", d=2), ALU.max).then_inc(s_max, 1)

                    alternate(dve, step)
                    largest(NG - 1, 0)
                    done[0] = base + 2 * NG

                    dve.wait_ge(s_edge, 32)
                    link(dve.tensor_copy(dst_rel[:, :], dst_i[:, :]))
                    by_chunk = dst_rel[:, :].rearrange("p (c k) -> p c k", k=K)
                    dve.tensor_reduce(lohi[:, 0, :], by_chunk, AX.X, ALU.min).then_inc(s_lohi, 1)
                    dve.tensor_reduce(lohi[:, 1, :], by_chunk, AX.X, ALU.max).then_inc(s_lohi, 1)
                    dve.wait_ge(s_max, NG)
                    dve.tensor_copy(ten[:, 0:8], tab_max[:, :, :].rearrange("p d h -> p (d h)")).then_inc(s_ten, 1)
                    for d in range(2):
                        dve.tensor_reduce(ten[:, 8 + d:9 + d], attr_all[:, d, :], AX.X, ALU.max,
                                          apply_absolute_value=True).then_inc(s_ten, 1)
                    dve.wait_ge(s_lohit, 1)
                    parts = p_a[0:NCB, :].rearrange("p (m b q) -> p m b q", m=2, b=2)
                    dve.tensor_reduce(lohi_c[0:NCB, 0:2], parts[:, 0], AX.X, ALU.min).then_inc(s_lohic, 1)
                    dve.tensor_reduce(lohi_c[0:NCB, 2:4], parts[:, 1], AX.X, ALU.max).then_inc(s_lohic, 1)
                    dve.wait_ge(s_tent, 1)
                    dve.tensor_reduce(ten_max[:, :], p_d[0:10, 0:P], AX.X, ALU.max).then_inc(s_tenc, 1)
                    dve.wait_ge(s_rows, 1)
                    dve.tensor_copy(row[:, 0:2, :], p_b[0:1, 0:2 * NCH].rearrange("p (m c) -> p m c", m=2))\
                       .then_inc(s_first, 1)
                    dve.wait_ge(s_first, 1)
                    link(dve.tensor_tensor(row[:, 1, :], row[:, 1, :], row[:, 0, :], ALU.subtract))
                    link(dve.tensor_copy(span[:, :], row[:, 1, :]))
                    link(dve.tensor_single_scalar(span[:, :], span[:, :], WSH, ALU.logical_shift_right))
                    link(dve.tensor_copy(row[:, 2, :], span[:, :]))
                    link(dve.memset(row[:, 1, :], 1.0))
                    link(dve.tensor_tensor_scan(row[:, 3, :], row[:, 1, :], row[:, 2, :], 0.0, ALU.mult, ALU.add))
                    link(dve.tensor_tensor(row[:, 3, :], row[:, 3, :], row[:, 2, :], ALU.subtract))
                    dve.tensor_copy(before[:, :], row[:, 3, :])
                    link(dve.scalar_tensor_tensor(out=row[:, 1, :], in0=row[:, 2, :], scalar=float(EXTRA),
                                                  in1=row[:, 0, :], op0=ALU.mult, op1=ALU.add))
                    dve.tensor_copy(windows[:, 1:1 + NCH], row[:, 1, :])
                    dve.wait_ge(s_firstb, 1)
                    dve.tensor_tensor(by_chunk, by_chunk, p_c[:, 0:NCH].unsqueeze(2).broadcast_to([P, NCH, K]),
                                      ALU.subtract)
                    dve.wait_ge(s_tenr, 1)
                    link(dve.tensor_copy(small[:, 10:16], p_d[0:1, P + 4:P + 10]))
                    link(dve.tensor_scalar(small[:, 0:4], p_d[0:1, P:P + 4], small[:, 14:15], None, ALU.mult))
                    link(dve.scalar_tensor_tensor(out=small[:, 4:8], in0=small[:, 10:14], scalar=small[:, 15:16],
                                                  in1=small[:, 0:4], op0=ALU.mult, op1=ALU.add))
                    link(dve.tensor_reduce(small[:, 8:9], small[:, 4:8], AX.X, ALU.max))
                    dve.tensor_scalar(small[:, 9:10], small[:, 8:9], -1.0, HEADROOM, ALU.mult, ALU.add)\
                       .then_inc(s_shift, 1)
                    dve.wait_ge(s_shiftb, 1)
                    dve.tensor_copy(neg_shift[:, :], p_d[:, 2 * P:2 * P + 1])

        with ExitStack() as ctx:
            sb, ps, sem = tensors(ctx)
            part = sb("part", [P, 2, K, COLS])
            msg = sb("msg", [P, 2, K, COLS])
            score = sb("score", [P, 2, K, HEADS])
            ex = sb("ex", [P, 2, K, HEADS])
            val = sb("val", [P, 2, K, HEADS * HD])
            hot = sb("hot", [P, 2, K, W])
            hot_x = sb("hot_x", [P, K, W])
            iota_x = sb("iota_x", [P, W])
            p_win = ps("p_win", [P, 2, 512])
            p_x = ps("p_x", [P, 512])

            turns = sem("pool_turns")
            rows_used = sem("rows_used")
            parts_ready = sem("parts_ready")
            hot_ready = sem("hot_ready")
            max_taken = sem("max_taken")
            score_ready = sem("score_ready")
            exp_ready = sem("exp_ready")
            val_ready = sem("val_ready")
            summed = sem("window_summed")
            added = sem("window_added")
            x_hot = sem("extra_hot_ready")
            x_summed = sem("extra_window_summed")

            def chunks(eng, begin, step, begun=0):
                loaded = begin(0)
                for s in range(begun, RING):
                    step(s, s, 0, loaded)
                with eng.Fori(1, NIT) as it:
                    loaded = begin(it)
                    for s in range(RING):
                        step(it * RING + s, s, it, loaded)

            def load(eng, ap, most):
                return nc.values_load_multi_w_load_instructions(
                    ap, engines=[eng.engine], min_val=0, max_val=most)[1]

            def sum_window(pe, psum, v, one_hot):
                for b in range(2):
                    for k in range(K):
                        pe.matmul(psum[:, b * W:(b + 1) * W], val[:, v, k, b * P:(b + 1) * P], one_hot[:, k, :],
                                  start=(k == 0), stop=(k == K - 1))
                for k in range(K):
                    last = pe.matmul(psum[0:HEADS, 2 * W:3 * W], ex[:, v, k, :], one_hot[:, k, :],
                                     start=(k == 0), stop=(k == K - 1))
                return last

            with nc.Block() as block:
                @block.sync
                def _(sp):
                    def step(c, s, it, _):
                        after(sp, gathered[s], 16 * K * it)
                        sp.dma_start(index[:, s, :], src[c] if isinstance(c, int)
                                     else src[ds(c, 1)].rearrange("a p k -> (a p) k")).then_inc(index_ready[s], 16)

                    chunks(sp, lambda it: None, step, RING)

                @block.gpsimd
                def _(pool):
                    def step(c, s, it, _):
                        pool.wait_ge(index_ready[s], 16 * (it + 1))
                        after(pool, rows_used, c - RING + 1)
                        settle(pool, turns)
                        gather(pool, s)
                    chunks(pool, lambda it: None, step, EARLY)

                @block.scalar
                def _(act):
                    def step(c, s, it, _):
                        v = s % 2
                        act.wait_ge(score_ready, c + 1)
                        after(act, summed, c - 1)
                        act.activation(ex[:, v, :, :], score[:, v, :, :], ACT.Exp, bias=neg_shift[:, 0:1])\
                           .then_inc(exp_ready, 1)
                    chunks(act, lambda it: None, step)

                @block.tensor
                def _(pe):
                    def begin(it):
                        return load(pe, windows[:, ds(it * RING + 1, RING)], EXTRA * (MAXWIN + 1))

                    def step(c, s, it, loaded):
                        v = s % 2
                        pe.wait_ge(hot_ready, c + 1)
                        pe.wait_ge(val_ready, c + 1)
                        after(pe, added, c - 1)
                        sum_window(pe, p_win[:, v, :], v, hot[:, v, :, :]).then_inc(summed, 1)
                        with pe.If(loaded[s] > EXTRA - 1):
                            ahead, = load(pe, before[:, ds(c, 1)], NCH * MAXWIN)
                            with pe.Fori(0, loaded[s] >> 13) as j:
                                pe.wait_ge(x_hot, ahead + j + 1)
                                sum_window(pe, p_x[:, :], v, hot_x[:, :, :]).then_inc(x_summed, 1)
                            pe.nop()
                    chunks(pe, begin, step)

                @block.vector
                def _(dve):
                    def begin(it):
                        return load(dve, windows[:, ds(it * RING, RING + 1)], EXTRA * (MAXWIN + 1))

                    def first_of(word):
                        return nc.s_assert_within(word & (EXTRA - 1), 0, NP - 1)

                    def add_window(psum, node):
                        for a, b in ((acc[:, :, ds(node, W)], psum[:, 0:2 * W].rearrange("p (b w) -> p b w", b=2)),
                                     (acc_e[:, ds(node, W)], psum[0:HEADS, 2 * W:3 * W])):
                            last = dve.tensor_tensor(a, a, b, ALU.add)
                        return last

                    def step(c, s, it, loaded):
                        v = s % 2
                        per_edge = attr_all[:, :, ds(c * K, K)]
                        dve.wait_ge(gathered[s], 16 * K * (it + 1))
                        for d in range(2):
                            last = dve.tensor_tensor(
                                part[:, d, :, :], rows[:, s, :, d * COLS:(d + 1) * COLS],
                                per_edge[:, d, :].unsqueeze(2).broadcast_to([P, K, COLS]), ALU.mult)
                        last.then_inc(parts_ready, 1)
                        after(dve, summed, c - 1)
                        dve.wait_ge(parts_ready, c + 1)
                        dve.tensor_tensor(msg[:, v, :, :], part[:, 0, :, :], part[:, 1, :, :], ALU.add)\
                           .then_inc(rows_used, 1)
                        dve.wait_ge(rows_used, c + 1)
                        raw = msg[:, v, :, HD:COLS]
                        dve.scalar_tensor_tensor(out=score[:, v, :, :], in0=raw, scalar=0.2, in1=raw, op0=ALU.mult,
                                                 op1=ALU.max).then_inc(score_ready, 1)
                        dve.tensor_tensor(hot[:, v, :, :],
                                          dst_rel[:, ds(c * K, K)].unsqueeze(2).broadcast_to([P, K, W]),
                                          iota_w[:, :].unsqueeze(1).broadcast_to([P, K, W]), ALU.is_equal)\
                           .then_inc(hot_ready, 1)
                        dve.wait_ge(score_ready, c + 1)
                        after(dve, max_taken, c)
                        dve.tensor_tensor(run_max[:, :, :], run_max[:, :, :], score[:, v, :, :], ALU.max)\
                           .then_inc(max_taken, 1)
                        dve.wait_ge(exp_ready, c + 1)
                        dve.tensor_tensor(
                            val[:, v, :, :].rearrange("p k (h f) -> p k h f", h=HEADS),
                            msg[:, v, :, 0:HD].unsqueeze(2).broadcast_to([P, K, HEADS, HD]),
                            ex[:, v, :, :].unsqueeze(3).broadcast_to([P, K, HEADS, HD]), ALU.mult)\
                           .then_inc(val_ready, 1)
                        if not isinstance(c, int) or c > 0:
                            finish(c - 1, (s - 1) % RING, loaded[s])
                        extra_windows(c, s, loaded[s + 1])

                    def finish(c, s, word):
                        dve.wait_ge(summed, c + 1)
                        after(dve, added, c)
                        add_window(p_win[:, s % 2, :], first_of(word)).then_inc(added, 1)

                    def extra_windows(c, s, word):
                        with dve.If(word > EXTRA - 1):
                            ahead, = load(dve, before[:, ds(c, 1)], NCH * MAXWIN)
                            dve.tensor_copy(iota_x[:, :], iota_w[:, :])
                            dve.drain()
                            with dve.Fori(0, word >> 13) as j:
                                dve.tensor_scalar(iota_x[:, :], iota_x[:, :], float(W), None, ALU.add)
                                dve.drain()
                                dve.tensor_tensor(hot_x[:, :, :],
                                                  dst_rel[:, ds(c * K, K)].unsqueeze(2).broadcast_to([P, K, W]),
                                                  iota_x[:, :].unsqueeze(1).broadcast_to([P, K, W]), ALU.is_equal)\
                                   .then_inc(x_hot, 1)
                                dve.wait_ge(x_summed, ahead + j + 1)
                                node = nc.s_assert_within(first_of(word) + j * W + W, 0, NP - 1)
                                add_window(p_x[:, :], node)
                                dve.drain()
                            dve.nop()
                    chunks(dve, begin, step)
                    final, = load(dve, windows[:, NCH:NCH + 1], EXTRA * (MAXWIN + 1))
                    finish(NCH - 1, RING - 1, final)


def stage_nodes(nc, tensors, g):
    token_rows, top_w, expert_f, expert_of_tile, row_of_tile, more_turns, run_end, pad_row, residual, dispatched = (
        g[n] for n in ("token_rows", "top_w", "expert_f", "expert_of_tile", "row_of_tile", "more_turns", "run_end",
                       "pad_row", "residual", "dispatched"))
    ident, ones, eps, acc, acc_e, run_max, neg_shift, sent = (
        g[n] for n in ("ident", "ones", "eps", "acc", "acc_e", "run_max", "neg_shift", "sent"))
    G = 2 * U
    with ExitStack() as ctx:
        sb, ps, sem = tensors(ctx)
        gate_w = sb("gate_w", [P, KC, E])
        gate_b = sb("gate_b", [P, E])
        head_max = sb("head_max", [P, HEADS])
        top4 = sb("top4", [HEADS, 1])
        eps4 = sb("eps4", [HEADS, 1])
        diag4 = sb("diag4", [HEADS, HEADS])
        eps_b = sb("eps_b", [P, HEADS])
        inv = sb("inv", [P, NT, HEADS])
        staged = sb("staged", [P, U, 2, P])
        attn = sb("attn", [P, U, D])
        x1 = sb("x1", [P, 2, U, D])
        stats = sb("stats3", [P, U, 6])
        mv = sb("mv3", [P, U, 2])
        rstd = sb("rstd3", [P, U])
        nmr = sb("nmr3", [P, U])
        xn = sb("xn3", [P, 2, U, XROW])
        xt = sb("xt3", [P, 2, KC, P])
        logits = sb("logits", [P, U, E])
        best = sb("best", [P, U, 8])
        best_i = sb("best_i", [P, U, 8], U32)
        top_v = sb("top_v", [P, NT, 2])
        top_g = sb("top_g", [P, U, 2])
        token = sb("token", [P, U])
        earlier = sb("earlier", [P, P], BF16)
        ones_b = sb("ones_b", [P, P], BF16)
        iota_e = sb("iota_e", [P, E])
        iota_m = sb("iota_m", [P, NT])
        iota_j = sb("iota_j", [P, NJ])
        region = sb("region", [P, E])
        pad_expert = sb("pad_expert", [P, 1])
        pad_far = sb("pad_far", [P, 1])
        takes = sb("takes", [P, E, G], BF16)
        total = sb("total", [P, E, 1 + G])
        carry = sb("carry", [P, E, 1 + G])
        restart = sb("restart", [P, E, 1 + G])
        place = sb("place", [P, E, G])
        slot_f = sb("slot_f", [P, G])
        slot_i = sb("slot_i", [P, 2, G], I32)
        many = sb("many", [P, E, NT])
        ntile = sb("ntile", [P, E])
        ends = sb("ends", [P, E])
        cmp = sb("cmp", [P, NJ, E])
        start = sb("start", [P, NJ])
        turn_f = sb("turn_f", [P, NJ // R5])
        turns_f = sb("turns_f", [P, 1])
        row_f = sb("row_f", [P, NJ])
        gap = sb("gap", [P, NT])

        p_g = ps("p_g", [P, U + 1, D])
        p_t = ps("p_t", [P, 2, 512])
        p_l = ps("p_l", [P, 512])
        p_n = ps("p_n", [P, 2, 256])
        p_s, p_e = p_l, p_n[:, 0, :]

        s_in = sem("router_loaded")
        s_hm = sem("head_max_ready")
        s_hmt = sem("head_max_transposed")
        s_top = sem("score_max_ready")
        s_eps = sem("eps_scaled")
        s_diag = sem("eps_diagonal")
        s_epsb = sem("eps_broadcast")
        s_et = sem("exp_sums_transposed")
        s_chain = sem("dve_steps3")
        s_st = sem("staged")
        s_gt = sem("sums_transposed")
        s_attn = sem("attention_ready")
        s_x1 = sem("residual_added")
        s_bn = sem("stats_ready3")
        s_mv = sem("mean_var_ready3")
        s_sd = sem("deviation_ready3")
        s_rc = sem("rstd_ready3")
        s_nm = sem("normalised3")
        s_xt = sem("rows_transposed3")
        s_xc = sem("rows_t_copied3")
        s_l = sem("logits_summed")
        s_lg = sem("logits_ready")
        s_best = sem("best_ready")
        s_besti = sem("best_index_ready")
        s_top2 = sem("best_kept")
        s_take = sem("takes_ready")
        s_pre = sem("counts_summed")
        s_tot = sem("totals_copied")
        s_slot = sem("slot_steps")
        s_ready = sem("slots_ready")
        s_out = [sem("residual_stored0"), sem("residual_stored1")]
        s_kept = [sem("rows_kept0"), sem("rows_kept1")]
        s_c = sem("constants3")
        s_c2 = sem("constants3_chain")
        s_run = sem("run_ends_ready")
        s_pad = sem("padding_written")
        s_gap = sem("logit_gap")
        s_exp = sem("second_exp")
        turns = sem("dve_turns3")
        pool_turns = sem("pool_turns3")

        def final(i):
            return isinstance(i, int) and i == NG - 1

        def first(i):
            return isinstance(i, int) and i == 0

        with nc.Block() as block:
            @block.sync
            def _(sp):
                sp.dma_start(gate_w[:, :, :], g["gate_w"].rearrange("(c p) e -> p c e", p=P)).then_inc(s_in, 16)
                sp.dma_start(gate_b[:, :], g["gate_b"].partition_broadcast(P)).then_inc(s_in, 16)
                rv = residual.rearrange("(g u p) d -> g p u d", p=P, u=U)

                def step(i, v, k):
                    sp.wait_ge(s_x1, (i + 1) * U)
                    sp.dma_start(rv[i] if isinstance(i, int) else
                                 rv[ds(i, 1)].rearrange("g p u d -> (g p) u d"), x1[:, v, :, :])\
                      .then_inc(s_out[v], 16)
                    sp.wait_ge(s_nm, (i + 1) * U)
                    sp.dma_start(token_rows[:, ds(i * U, U), :], xn[:, v, :, 0:D]).then_inc(s_kept[v], 16)
                alternate(sp, step)
                for v in range(2):
                    sp.wait_ge(s_out[v], 16 * ((NG + 1 - v) // 2))
                sp.wait_ge(s_run, 1)
                sp.wait_ge(s_c, CONSTANTS)
                for e in range(0, E, 4):
                    rows = nc.values_load_multi_w_load_instructions(
                        run_end[:, e:e + 4], engines=[sp.engine], min_val=0, max_val=SLOTS - P)[1]
                    for row in rows:
                        sp.dma_start(dispatched[ds(row, P), :], pad_row[:, :]).then_inc(s_pad, 16)
                sp.dma_start(dispatched[E * CAP:SLOTS, :], pad_row[:, :]).then_inc(s_pad, 16)
                for v in range(2):
                    sp.wait_ge(s_kept[v], 16 * ((NG + 1 - v) // 2))
                sp.wait_ge(s_pad, 16 * (E + 1))

            @block.gpsimd
            def _(pool):
                pool.memset(earlier[:, :], 1.0).then_inc(s_c2, 1)
                pool.memset(pad_expert[:, :], float(E)).then_inc(s_c2, 1)
                pool.memset(pad_far[:, :], FAR).then_inc(s_c2, 1)
                pool.memset(restart[:, :, :], 1.0).then_inc(s_c2, 1)
                pool.memset(pad_row[:, 0:D], 0.0).then_inc(s_c, 1)
                pool.memset(pad_row[:, D:XROW], FAR).then_inc(s_c, 1)
                pool.memset(ones_b[:, :], 1.0).then_inc(s_c, 1)
                for tile, n, by, rows in ((iota_e, E, 1, 0), (iota_m, NT, P, 0), (iota_j, NJ, 1, 0),
                                          (region, E, CAP, 0), (token, U, P, 1)):
                    pool.iota(tile[:, :], pattern=[[by, n]], base=0, channel_multiplier=rows,
                              allow_small_or_imprecise_dtypes=True).then_inc(s_c, 1)
                pool.iota(total[:, :, 0], pattern=[[CAP, E]], base=0, channel_multiplier=0,
                          allow_small_or_imprecise_dtypes=True).then_inc(s_c, 1)
                pool.wait_ge(s_c2, 4)
                pool.affine_select(out=earlier[:, :], in_=earlier[:, :], compare_op=ALU.is_gt, fill=0.0,
                                   base=0, pattern=[[1, P]], channel_multiplier=-1).then_inc(s_c, 1)
                for pad in (pad_expert, pad_far):
                    pool.affine_select(out=pad[:, :], in_=pad[:, :], compare_op=ALU.is_ge, fill=0.0,
                                       base=-LAST, pattern=[[0, 1]], channel_multiplier=1).then_inc(s_c, 1)
                pool.memset(restart[:, :, 0:1], 0.0).then_inc(s_c, 1)
                def step(i, v, k):
                    if not first(i):
                        dispatch(i - 1, 1 - v)

                def dispatch(i, v):
                    pool.wait_ge(s_nm, (i + 1) * U)
                    pool.wait_ge(s_ready, i + 1)
                    settle(pool, pool_turns)
                    for n in range(G):
                        pool.indirect_dma_start(
                            out=dispatched, out_offset=bass.IndirectOffsetOnAxis(ap=slot_i[:, v, n:n + 1], axis=0),
                            in_=xn[:, v, n // 2, :], in_offset=None, bounds_check=SLOTS - 1, oob_is_err=False)\
                            .then_inc(sent[v], 16)
                alternate(pool, step)
                dispatch(NG - 1, 0)

            @block.scalar
            def _(act):
                act.wait_ge(s_top, 1)
                act.activation(eps4[:, :], top4[:, :], ACT.Exp, bias=neg_shift[0:HEADS, 0:1]).then_inc(s_eps, 1)

                def stage(i):
                    for u in range(U):
                        t = i * U + u
                        after(act, s_gt, t - U + 1)
                        act.activation(staged[:, u, :, :], acc[:, :, ds(t * P, P)], ACT.Copy).then_inc(s_st, 1)

                def totals(i):
                    act.wait_ge(s_pre, i + 1)
                    after(act, s_slot, STEPS * i)
                    act.activation(total[:, :, 1:1 + G], p_n[:, 1, 0:E * G].rearrange("p (e g) -> p e g", g=G),
                                   ACT.Copy).then_inc(s_tot, 1)

                def step(i, v, k):
                    if not final(i):
                        stage(i + 1)
                    if not first(i):
                        totals(i - 1)
                    act.wait_ge(s_rc, 2 * i + 2)
                    after(act, s_kept[v], 16 * k)
                    after(act, sent[v], 16 * G * k)
                    for u in range(U):
                        act.activation(xn[:, v, u, 0:D], x1[:, v, u, :], ACT.Identity,
                                       bias=nmr[:, u:u + 1], scale=rstd[:, u:u + 1]).then_inc(s_nm, 1)
                    for u in range(U):
                        t = i * U + u
                        act.wait_ge(s_xt, t + 1)
                        after(act, s_l, t - reuse(u, 2, U) + 1)
                        act.activation(xt[:, u % 2, :, :],
                                       p_t[:, u % 2, 0:D].rearrange("p (c n) -> p c n", c=KC), ACT.Copy)\
                           .then_inc(s_xc, 1)
                    if not final(i):
                        deviation(i + 1)

                def deviation(i):
                    act.wait_ge(s_mv, i + 1)
                    act.activation(rstd[:, :], mv[:, :, 1], ACT.Sqrt, bias=eps[:, 0:1]).then_inc(s_sd, 1)
                stage(0)
                deviation(0)
                alternate(act, step)
                totals(NG - 1)
                act.wait_ge(s_gap, 1)
                act.activation(gap[:, :], gap[:, :], ACT.Exp).then_inc(s_exp, 1)

            @block.tensor
            def _(pe):
                pe.wait_ge(s_hm, 1)
                pe.transpose(p_s[0:HEADS, 0:P], head_max[:, :], ident[:, :]).then_inc(s_hmt, 1)
                for t in range(NT):
                    last = pe.transpose(p_e[:, t * HEADS:(t + 1) * HEADS], acc_e[:, t * P:(t + 1) * P],
                                        ident[0:HEADS, 0:HEADS])
                last.then_inc(s_et, 1)
                pe.wait_ge(s_diag, 1)
                pe.matmul(p_s[:, P:P + HEADS], ones[0:HEADS, :], diag4[:, :], start=True, stop=True)\
                  .then_inc(s_epsb, 1)
                pe.wait_ge(s_in, 32)
                pe.wait_ge(s_c, CONSTANTS)

                def sums(i):
                    after(pe, s_attn, i * U)
                    for u in range(U):
                        t = i * U + u
                        pe.wait_ge(s_st, t + 1)
                        for b in range(2):
                            last = pe.transpose(p_g[:, u, b * P:(b + 1) * P], staged[:, u, b, :], ident[:, :])
                        last.then_inc(s_gt, 1)

                def counts(i):
                    pe.wait_ge(s_take, i + 1)
                    after(pe, s_tot, i)
                    after(pe, s_slot, STEPS * i)
                    flat = takes[:, :, :].rearrange("p e g -> p (e g)")
                    pe.matmul(p_n[:, 0, 0:E * G], earlier[:, :], flat, start=True, stop=True)
                    pe.matmul(p_n[:, 1, 0:E * G], ones_b[:, :], flat, start=True, stop=True).then_inc(s_pre, 1)

                def product(i, u):
                    t = i * U + u
                    pe.wait_ge(s_xc, t + 1)
                    for c in range(KC):
                        last = pe.matmul(p_l[:, u * E:(u + 1) * E], xt[:, u % 2, c, :], gate_w[:, c, :],
                                         start=(c == 0), stop=(c == KC - 1))
                    last.then_inc(s_l, 1)

                def step(i, v, k):
                    if not final(i):
                        sums(i + 1)
                    if not first(i):
                        counts(i - 1)
                    after(pe, s_lg, i)
                    for u in range(U):
                        t = i * U + u
                        pe.wait_ge(s_nm, t + 1)
                        after(pe, s_xc, t - reuse(u, 2, U) + 1)
                        for c in range(KC):
                            last = pe.transpose(p_t[:, u % 2, c * P:(c + 1) * P],
                                                xn[:, v, u, c * P:(c + 1) * P], ident[:, :])
                        last.then_inc(s_xt, 1)
                        if u:
                            product(i, u - 1)
                    product(i, U - 1)
                sums(0)
                alternate(pe, step)
                counts(NG - 1)

            @block.vector
            def _(dve):
                dve.tensor_reduce(head_max[:, :], run_max[:, :, :].rearrange("p k h -> p h k"), AX.X, ALU.max)\
                   .then_inc(s_hm, 1)
                dve.wait_ge(s_hmt, 1)
                dve.tensor_reduce(top4[:, :], p_s[0:HEADS, 0:P], AX.X, ALU.max).then_inc(s_top, 1)
                dve.wait_ge(s_eps, 1)
                dve.tensor_scalar(diag4[:, :], ident[0:HEADS, 0:HEADS], eps4[:, 0:1], 1e-10, ALU.mult, ALU.mult)\
                   .then_inc(s_diag, 1)
                dve.wait_ge(s_epsb, 1)
                done = [0]

                def link(ins):
                    done[0] += 1
                    ins.then_inc(s_chain, 1)
                    dve.wait_ge(s_chain, done[0])

                link(dve.tensor_copy(eps_b[:, :], p_s[:, P:P + HEADS]))
                dve.wait_ge(s_et, 1)
                link(dve.tensor_tensor(inv[:, :, :], p_e[:, 0:NT * HEADS].rearrange("p (t h) -> p t h", h=HEADS),
                                       eps_b[:, :].unsqueeze(1).broadcast_to([P, NT, HEADS]), ALU.add))
                link(dve.reciprocal(inv[:, :, :], inv[:, :, :]))
                dve.wait_ge(s_in, 32)
                dve.wait_ge(s_c, CONSTANTS)

                def attention(i, v, k):
                    dve.wait_ge(s_gt, (i + 1) * U)
                    for u in range(U):
                        t = i * U + u
                        after(dve, s_x1, t - U + 1)
                        dve.tensor_tensor(attn[:, u, :].rearrange("p (h f) -> p h f", h=HEADS),
                                          p_g[:, u, :].rearrange("p (h f) -> p h f", h=HEADS),
                                          inv[:, ds(t, 1), :].rearrange("p a h -> p (a h)").unsqueeze(2)
                                          .broadcast_to([P, HEADS, HD]), ALU.mult).then_inc(s_attn, 1)
                    after(dve, s_nm, (i - 1) * U)
                    after(dve, s_out[v], 16 * k)
                    for u in range(U):
                        t = i * U + u
                        dve.wait_ge(s_attn, t + 1)
                        dve.tensor_tensor(x1[:, v, u, :], attn[:, u, :], tile_row(token_rows, t), ALU.add)\
                           .then_inc(s_x1, 1)

                def slots(i, v):
                    n = [0]

                    def next_step(ins):
                        n[0] += 1
                        ins.then_inc(s_slot, 1)
                        dve.wait_ge(s_slot, i * STEPS + n[0])

                    dve.wait_ge(s_tot, i + 1)
                    next_step(dve.tensor_tensor_scan(carry[:, :, :].rearrange("p e g -> p (e g)"),
                                                     restart[:, :, :].rearrange("p e g -> p (e g)"),
                                                     total[:, :, :].rearrange("p e g -> p (e g)"), 0.0,
                                                     ALU.mult, ALU.add))
                    next_step(dve.tensor_tensor(place[:, :, :], carry[:, :, 0:G],
                                                p_n[:, 0, 0:E * G].rearrange("p (e g) -> p e g", g=G), ALU.add))
                    next_step(dve.tensor_copy(total[:, :, 0:1], carry[:, :, G:G + 1]))
                    next_step(dve.tensor_tensor(place[:, :, :], place[:, :, :], takes[:, :, :], ALU.mult))
                    after(dve, s_ready, i)
                    next_step(dve.tensor_reduce(slot_f[:, :], place[:, :, :].rearrange("p e g -> p g e"), AX.X,
                                                ALU.add))
                    assert n[0] == STEPS
                    if final(i):
                        link(dve.tensor_scalar(slot_f[:, G - 2:G], slot_f[:, G - 2:G], pad_far[:, 0:1], None, ALU.add))
                    dve.tensor_copy(slot_i[:, v, :], slot_f[:, :]).then_inc(s_ready, 1)

                def best_two(i, v, k):
                    dve.wait_ge(s_l, (i + 1) * U)
                    dve.tensor_tensor(logits[:, :, :], p_l[:, 0:U * E].rearrange("p (u e) -> p u e", e=E),
                                      gate_b[:, :].unsqueeze(1).broadcast_to([P, U, E]), ALU.add)\
                       .then_inc(s_lg, 1)
                    dve.wait_ge(s_lg, i + 1)
                    settle(dve, turns)
                    for u in range(U):
                        last = dve.max(best[:, u, :], logits[:, u, :])
                    last.then_inc(s_best, 1)
                    dve.wait_ge(s_best, i + 1)
                    settle(dve, turns)
                    for u in range(U):
                        last = dve.max_index(best_i[:, u, :], best[:, u, :], logits[:, u, :])
                    last.then_inc(s_besti, 1)
                    dve.wait_ge(s_besti, i + 1)
                    dve.tensor_copy(top_v[:, ds(i * U, U), :], best[:, :, 0:2])
                    dve.tensor_copy(top_g[:, :, :], best_i[:, :, 0:2]).then_inc(s_top2, 1)
                    dve.wait_ge(s_top2, 2 * i + 1)
                    if final(i):
                        link(dve.tensor_scalar(top_g[:, U - 1, :], top_g[:, U - 1, :], pad_expert[:, 0:1], None,
                                               ALU.add))
                    dve.tensor_tensor(takes[:, :, :],
                                      top_g[:, :, :].rearrange("p u k -> p (u k)").unsqueeze(1)
                                      .broadcast_to([P, E, G]),
                                      iota_e[:, :].unsqueeze(2).broadcast_to([P, E, G]), ALU.is_equal)\
                       .then_inc(s_take, 1)
                    after(dve, sent[v], 16 * G * k)
                    dve.tensor_copy(xn[:, v, :, D + 1], top_g[:, :, 1])
                    dve.tensor_copy(xn[:, v, :, D], token[:, :]).then_inc(s_top2, 1)
                    dve.wait_ge(s_top2, 2 * i + 2)
                    dve.tensor_scalar(token[:, :], token[:, :], float(U * P), None, ALU.add)

                def statistics(i, v):
                    for u in range(U):
                        dve.wait_ge(s_x1, i * U + u + 1)
                        last = dve.bn_stats(stats[:, u, :], x1[:, v, u, :])
                    last.then_inc(s_bn, 1)
                    dve.wait_ge(s_bn, i + 1)
                    after(dve, s_nm, i * U)
                    settle(dve, turns)
                    for u in range(U):
                        last = dve.bn_aggr(mv[:, u, :], stats[:, u, :])
                    last.then_inc(s_mv, 1)

                def inverse(i):
                    dve.wait_ge(s_sd, i + 1)
                    dve.reciprocal(rstd[:, :], rstd[:, :]).then_inc(s_rc, 1)
                    dve.wait_ge(s_rc, 2 * i + 1)
                    dve.scalar_tensor_tensor(out=nmr[:, :], in0=mv[:, :, 0], scalar=-1.0, in1=rstd[:, :],
                                             op0=ALU.mult, op1=ALU.mult).then_inc(s_rc, 1)

                def step(i, v, k):
                    if not first(i):
                        slots(i - 1, 1 - v)
                    if not final(i):
                        attention(i + 1, 1 - v, k + v)
                        statistics(i + 1, 1 - v)
                    best_two(i, v, k)
                    if not final(i):
                        inverse(i + 1)
                attention(0, 0, 0)
                statistics(0, 0)
                inverse(0)
                alternate(dve, step)
                slots(NG - 1, 0)

                dve.tensor_tensor(gap[:, :], top_v[:, :, 1], top_v[:, :, 0], ALU.subtract).then_inc(s_gap, 1)
                dve.tensor_copy(run_end[:, :], total[0:1, :, 0]).then_inc(s_run, 1)
                link(dve.tensor_tensor(region[:, :], total[:, :, 0], region[:, :], ALU.subtract))
                link(dve.tensor_tensor(many[:, :, :], region[:, :].unsqueeze(2).broadcast_to([P, E, NT]),
                                       iota_m[:, :].unsqueeze(1).broadcast_to([P, E, NT]), ALU.is_gt))
                link(dve.tensor_reduce(ntile[:, :], many[:, :, :], AX.X, ALU.add))
                link(dve.tensor_tensor_scan(ends[:, :], ones[:, 0:E], ntile[:, :], 0.0, ALU.mult, ALU.add))
                by_tile = ends[:, :].unsqueeze(1).broadcast_to([P, NJ, E])
                link(dve.tensor_tensor(cmp[:, :, :], by_tile, iota_j[:, :].unsqueeze(2).broadcast_to([P, NJ, E]),
                                       ALU.is_le))
                link(dve.tensor_reduce(expert_f[:, :], cmp[:, :, :], AX.X, ALU.add))
                link(dve.tensor_tensor(cmp[:, :, :], cmp[:, :, :], by_tile, ALU.mult))
                link(dve.tensor_reduce(start[:, :], cmp[:, :, :], AX.X, ALU.max))
                link(dve.tensor_tensor(start[:, :], iota_j[:, :], start[:, :], ALU.subtract))
                link(dve.tensor_scalar(row_f[:, :], expert_f[:, :], float(CAP), None, ALU.mult))
                link(dve.scalar_tensor_tensor(out=row_f[:, :], in0=start[:, :], scalar=float(P), in1=row_f[:, :],
                                              op0=ALU.mult, op1=ALU.add))
                link(dve.tensor_scalar(row_f[:, :], row_f[:, :], float(E * CAP), None, ALU.min))
                link(dve.tensor_scalar(expert_f[:, :], expert_f[:, :], float(E - 1), None, ALU.min))
                link(dve.tensor_scalar(turn_f[:, :], iota_j[:, 0:NJ // R5], float(R5), None, ALU.mult))
                link(dve.tensor_tensor(turn_f[:, :], ends[:, E - 1:E].broadcast_to([P, NJ // R5]), turn_f[:, :],
                                       ALU.is_gt))
                link(dve.tensor_reduce(turns_f[:, :], turn_f[:, :], AX.X, ALU.add))
                link(dve.tensor_scalar(turns_f[:, :], turns_f[:, :], -2.0, None, ALU.add))
                dve.tensor_copy(more_turns[:, :], turns_f[0:1, :])
                dve.tensor_copy(expert_of_tile[:, :], expert_f[0:1, :])
                dve.tensor_copy(row_of_tile[:, :], row_f[0:1, :])
                dve.wait_ge(s_exp, 1)
                link(dve.tensor_scalar(top_w[:, :, 1], gap[:, :], 1.0, None, ALU.add))
                link(dve.reciprocal(top_w[:, :, 0], top_w[:, :, 1]))
                link(dve.tensor_tensor(top_w[:, :, 1], gap[:, :], top_w[:, :, 0], ALU.mult))


def stage_experts(nc, tensors, g):
    token_rows, top_w, expert_of_tile, row_of_tile, more_turns, expert_f, sent = (
        g[n] for n in ("token_rows", "top_w", "expert_of_tile", "row_of_tile", "more_turns", "expert_f", "sent"))
    ident, eps, dispatched, expert_rows, residual = (
        g[n] for n in ("ident", "eps", "dispatched", "expert_rows", "residual"))

    with ExitStack() as ctx:
        sb, ps, sem = tensors(ctx)
        w1_sb = sb("w1_sb", [P, E, KC, F])
        w2_sb = sb("w2_sb", [P, E, FC, D])
        b1_sb = sb("b1_sb", [P, E * FC])
        second = sb("second", [P, R5])
        back = sb("back", [P, R5, 1], I32)
        xs = sb("xs", [P, R5, XROW])
        xt = sb("xt4", [P, 2, KC, P])
        hid = sb("hid", [P, 2, F])
        hid_t = sb("hid_t", [P, 2, FC, P])
        b2_t = sb("b2_t", [P, R5, D])
        ys = sb("ys", [P, R5, D])
        p_x = ps("p_x4", [P, 2, 512])
        p_h = ps("p_h", [P, 2, 512])
        p_ht = ps("p_ht", [P, 2, 512])
        p_y = ps("p_y", [P, 2, 512])

        turns = sem("pool_turns4")
        s_b1 = sem("hidden_biases")
        s_w = sem("expert_weights")
        s_second = sem("second_known")
        s_xs = [sem(f"xs_loaded{u}") for u in range(R5)]
        s_b2 = [sem(f"b2_loaded{u}") for u in range(R5)]
        s_t = sem("xs_transposed")
        s_tc = sem("xt_copied")
        s_h = sem("hidden_summed")
        s_hc = sem("hidden_copied")
        s_ht = sem("hidden_transposed")
        s_r = sem("relu_done")
        s_y = sem("result_summed")
        s_ys = sem("result_ready")
        s_bi = sem("back_index_ready")
        s_gone = [sem(f"result_scattered{u}") for u in range(R5)]

        def turns_of(eng, step):
            more, = nc.values_load_multi_w_load_instructions(more_turns[:, :], engines=[eng.engine],
                                                             min_val=LEAST - 2, max_val=NJ // R5 - 2)[1]
            for r in range(R5):
                step(r, r, 0, False)
            with eng.Fori(1, more + 1) as i:
                for r in range(R5):
                    step(i * R5 + r, r, i, False)
            end = nc.s_assert_within(more + 1, LEAST - 1, NJ // R5 - 1)
            for r in range(R5):
                step(end * R5 + r, r, end, True)
            return more + 2

        def behind(r, last, ahead):
            return last and r + ahead >= R5

        def load(eng, of, i, first, n, most=E - 1):
            return nc.values_load_multi_w_load_instructions(
                of[:, ds(i * R5 + first, n)], engines=[eng.engine], min_val=0, max_val=most)[1]

        with nc.Block() as block:
            @block.gpsimd
            def _(pool):
                def step(j, r, i, last):
                    pool.wait_ge(s_bi, j + 1)
                    pool.wait_ge(s_ys, j + 1)
                    settle(pool, turns)
                    pool.indirect_dma_start(
                        out=expert_rows, out_offset=bass.IndirectOffsetOnAxis(ap=back[:, r, :], axis=0),
                        in_=ys[:, r, :], in_offset=None, bounds_check=2 * NP - 1, oob_is_err=False)\
                        .then_inc(s_gone[r], 16)
                n = turns_of(pool, step)
                for r in range(R5):
                    pool.wait_ge(s_gone[r], n * 16)

            @block.sync
            def _(sp):
                sp.dma_start(b1_sb[:, :], g["b1"]).then_inc(s_b1, 16)
                for e in range(E):
                    sp.dma_start(w1_sb[:, e, :, :], g["w1"][e].rearrange("(c p) f -> p c f", p=P)).then_inc(s_w, 16)
                    sp.wait_ge(s_w, 32 * e + 16)
                    sp.dma_start(w2_sb[:, e, :, :], g["w2"][e].rearrange("(c p) d -> p c d", p=P)).then_inc(s_w, 16)
                    sp.wait_ge(s_w, 32 * e + 32)

            @block.scalar
            def _(act):
                def rows_t(j, u):
                    act.wait_ge(s_t, j + 1)
                    after(act, s_h, j - 1)
                    act.activation(xt[:, u, :, :], p_x[:, u, 0:D].rearrange("p (c n) -> p c n", c=KC), ACT.Copy)\
                       .then_inc(s_tc, 1)

                def relu(j, u, e):
                    act.wait_ge(s_ht, j + 1)
                    after(act, s_y, j - 1)
                    for c in range(FC):
                        last = act.activation(hid_t[:, u, c, :], p_ht[:, u, c * P:(c + 1) * P], ACT.Relu,
                                              bias=b1_sb[:, ds(e * FC + c, 1)])
                    last.then_inc(s_r, 1)

                def fetch(j, r, e, row):
                    after(act, s_t, j - R5 + 1)
                    after(act, s_bi, j - R5 + 1)
                    act.dma_start(xs[:, r, :], dispatched[ds(row, P), :]).then_inc(s_xs[r], 16)
                    after(act, s_ys, j - R5 + 1)
                    act.dma_start(b2_t[:, r, :], g["b2"][ds(e, 1), :].rearrange("a d -> (a d)")
                                  .partition_broadcast(P)).then_inc(s_b2[r], 16)

                AHEAD = R5 - 1
                state = {}

                def step(j, r, i, last):
                    if r == 0:
                        state["e"] = load(act, expert_of_tile, i, 0, R5)
                    relu(j, r % 2, state["e"][r])
                    if not behind(r, last, 2):
                        rows_t(j + 2, r % 2)
                    if behind(r, last, AHEAD):
                        return
                    if r == 0:
                        n = 1 if last else R5
                        state["row"] = load(act, row_of_tile, i, AHEAD, n, E * CAP)
                    if r == 1:
                        state["next"] = load(act, expert_of_tile, i, R5, AHEAD)
                    fetch(j + AHEAD, (r + AHEAD) % R5, state["e"][AHEAD] if r == 0 else state["next"][r - 1],
                          state["row"][r])

                for v in range(2):
                    act.wait_ge(sent[v], 16 * 2 * U * ((NG + 1 - v) // 2))
                e0 = load(act, expert_of_tile, 0, 0, AHEAD)
                row0 = load(act, row_of_tile, 0, 0, AHEAD, E * CAP)
                for j in range(AHEAD):
                    fetch(j, j, e0[j], row0[j])
                rows_t(0, 0)
                rows_t(1, 1)
                act.wait_ge(s_b1, 16)
                turns_of(act, step)

            @block.tensor
            def _(pe):
                def rows_t(j, r, i):
                    pe.wait_ge(s_xs[r % R5], 16 * (i + r // R5 + 1))
                    after(pe, s_tc, j - 1)
                    for c in range(KC):
                        last = pe.transpose(p_x[:, r % 2, c * P:(c + 1) * P], xs[:, r % R5, c * P:(c + 1) * P],
                                            ident[:, :])
                    last.then_inc(s_t, 1)

                def first_layer(j, u, e):
                    pe.wait_ge(s_w, e * 32 + 32)
                    pe.wait_ge(s_tc, j + 1)
                    after(pe, s_hc, j - 1)
                    for c in range(KC):
                        last = pe.matmul(p_h[:, u, :], xt[:, u, c, :], w1_sb[:, ds(e, 1), c, :]
                                         .rearrange("p a f -> p (a f)"), start=(c == 0), stop=(c == KC - 1))
                    last.then_inc(s_h, 1)

                def hidden_t(j, u):
                    pe.wait_ge(s_hc, j + 1)
                    after(pe, s_r, j - 1)
                    for c in range(FC):
                        last = pe.transpose(p_ht[:, u, c * P:(c + 1) * P], hid[:, u, c * P:(c + 1) * P], ident[:, :])
                    last.then_inc(s_ht, 1)

                def second_layer(j, u, e):
                    pe.wait_ge(s_r, j + 1)
                    after(pe, s_ys, j - 1)
                    for c in range(FC):
                        last = pe.matmul(p_y[:, u, 0:D], hid_t[:, u, c, :], w2_sb[:, ds(e, 1), c, :]
                                         .rearrange("p a d -> p (a d)"), start=(c == 0), stop=(c == FC - 1))
                    last.then_inc(s_y, 1)

                rows_t(0, 0, 0)
                rows_t(1, 1, 0)
                first_layer(0, 0, load(pe, expert_of_tile, 0, 0, 1)[0])
                experts = [None]

                def step(j, r, i, last):
                    u = r % 2
                    if r == 0:
                        experts[0] = load(pe, expert_of_tile, i, 0, R5 if last else R5 + 1)
                    hidden_t(j, u)
                    if not behind(r, last, 1):
                        first_layer(j + 1, 1 - u, experts[0][r + 1])
                    if not behind(r, last, 2):
                        rows_t(j + 2, r + 2, i)
                    second_layer(j, u, experts[0][r])
                turns_of(pe, step)

            @block.vector
            def _(dve):
                def hidden(j, u):
                    dve.wait_ge(s_h, j + 1)
                    after(dve, s_ht, j - 1)
                    dve.tensor_copy(hid[:, u, :], p_h[:, u, :]).then_inc(s_hc, 1)

                def step(j, r, i, last):
                    if not behind(r, last, 1):
                        hidden(j + 1, 1 - r % 2)
                    after(dve, s_gone[r], 16 * i)
                    dve.wait_ge(s_xs[r], 16 * (i + 1))
                    dve.tensor_tensor(second[:, r:r + 1], xs[:, r, D + 1:XROW], expert_f[:, ds(j, 1)], ALU.is_equal)\
                       .then_inc(s_second, 1)
                    dve.wait_ge(s_second, j + 1)
                    dve.scalar_tensor_tensor(out=back[:, r, :], in0=second[:, r:r + 1], scalar=float(NP),
                                             in1=xs[:, r, D:D + 1], op0=ALU.mult, op1=ALU.add).then_inc(s_bi, 1)
                    dve.wait_ge(s_y, j + 1)
                    dve.wait_ge(s_b2[r], 16 * (i + 1))
                    dve.tensor_tensor(ys[:, r, :], p_y[:, r % 2, 0:D], b2_t[:, r, :], ALU.add).then_inc(s_ys, 1)
                hidden(0, 0)
                turns_of(dve, step)

    with ExitStack() as ctx:
        sb, ps, sem = tensors(ctx)
        gamma = sb("gamma", [P, D])
        y0 = sb("y0", [P, 2, U, D])
        y1 = sb("y1", [P, 2, U, D])
        beta = sb("beta", [P, D])
        res = sb("res", [P, 2, U, D])
        mix = sb("mix", [P, 2, U, D])
        norm = sb("norm", [P, 2, U, D])
        done = sb("done", [P, 2, U, D])
        stats = sb("stats5", [P, U, 6])
        mv = sb("mv5", [P, U, 2])
        rstd = sb("rstd5", [P, U])
        nmr = sb("nmr5", [P, U])
        s_g = sem("gamma_beta_loaded")
        s_rb = sem("beta_added")
        s_y0 = [sem(f"first_rows_loaded{v}") for v in range(2)]
        s_y1 = [sem(f"second_rows_loaded{v}") for v in range(2)]
        s_res = [sem(f"residual_loaded{v}") for v in range(2)]
        s_m0 = sem("first_choice_added")
        s_m1 = sem("second_choice_added")
        s_bn = sem("stats_ready5")
        s_mv = sem("mean_var_ready5")
        s_sd = sem("deviation_ready5")
        s_rc = sem("rstd_ready5")
        s_nm = sem("normalised5")
        s_gm = sem("gamma_applied")
        s_pgm = sem("gamma_applied_pool")
        s_f = sem("final_ready")
        s_out = [sem(f"final_stored{v}") for v in range(2)]
        turns = sem("dve_turns5")
        ON_DVE = 5
        last_k = NG // 2

        with nc.Block() as block:
            def tiles(i):
                return [(0, U, P)] if not final(i) else [(0, U - 1, P), (U - 1, 1, LAST)]

            def final(i):
                return isinstance(i, int) and i == NG - 1

            def dram(rows, i, u, n, real):
                if isinstance(i, int):
                    t = i * U + u
                    return rows[t * P:(t + n - 1) * P + real, :].rearrange("(u p) d -> p u d", p=real)
                return rows.rearrange("(g u p) d -> g p u d", p=P, u=U)[ds(i, 1)].rearrange("g p u d -> (g p) u d")

            @block.sync
            def _(sp):
                whole_groups = g["out"][0:(NG - 1) * U * P, :]

                def load(i, v):
                    after(sp, s_m1, (i - 1) * U)
                    for u, n, real in tiles(i):
                        for to, of, loaded in ((y0, expert_rows[0:NP], s_y0), (y1, expert_rows[NP:2 * NP], s_y1)):
                            sp.dma_start(to[0:real, v, u:u + n, :], dram(of, i, u, n, real)).then_inc(loaded[v], 16)

                def load_residual(i, v):
                    after(sp, s_f, (i - 1) * U)
                    for u, n, real in tiles(i):
                        sp.dma_start(res[0:real, v, u:u + n, :], dram(residual, i, u, n, real)).then_inc(s_res[v], 16)

                def store(i, v):
                    sp.wait_ge(s_f, (i + 1) * U)
                    for u, n, real in tiles(i):
                        to = g["out"] if isinstance(i, int) else whole_groups
                        sp.dma_start(dram(to, i, u, n, real), done[0:real, v, u:u + n, :]).then_inc(s_out[v], 16)

                def step(i, v, k):
                    load(i, v)
                    if isinstance(i, int) and i == 0:
                        sp.dma_start(gamma[:, :], g["gamma"].partition_broadcast(P)).then_inc(s_g, 16)
                        sp.dma_start(beta[:, :], g["beta"].partition_broadcast(P)).then_inc(s_g, 16)
                    if not (isinstance(i, int) and i < 2):
                        store(i - 2, v)
                    load_residual(i, v)
                alternate(sp, step)
                store(NG - 2, 1)
                store(NG - 1, 0)
                sp.wait_ge(s_out[0], 16 * (last_k + 2))
                sp.wait_ge(s_out[1], 16 * last_k)

            @block.scalar
            def _(act):
                def step(i, v, k):
                    act.wait_ge(s_mv, i + 1)
                    act.activation(rstd[:, :], mv[:, :, 1], ACT.Sqrt, bias=eps[:, 0:1]).then_inc(s_sd, 1)
                    act.wait_ge(s_rc, 2 * i + 2)
                    after(act, s_f, (i - 1) * U)
                    for u in range(U):
                        act.activation(norm[:, v, u, :], mix[:, v, u, :], ACT.Identity, bias=nmr[:, u:u + 1],
                                       scale=rstd[:, u:u + 1]).then_inc(s_nm, 1)
                alternate(act, step)

            @block.gpsimd
            def _(pool):
                pool.wait_ge(s_g, 32)
                on_pool = U - ON_DVE

                def step(i, v, k):
                    pool.wait_ge(s_res[v], 16 * (k + 1) if not final(i) else 16 * (k + 2))
                    for u in range(U):
                        pool.tensor_tensor(res[:, v, u, :], res[:, v, u, :], beta[:, :], ALU.add).then_inc(s_rb, 1)
                    for u in range(ON_DVE, U):
                        pool.wait_ge(s_nm, i * U + u + 1)
                        pool.tensor_tensor(norm[:, v, u, :], norm[:, v, u, :], gamma[:, :], ALU.mult)\
                            .then_inc(s_pgm, 1)
                    after(pool, s_out[v], 16 * k)
                    for u in range(U):
                        pool.wait_ge(s_rb, i * U + u + 1)
                        if u < ON_DVE:
                            pool.wait_ge(s_gm, i * ON_DVE + u + 1)
                        else:
                            pool.wait_ge(s_pgm, i * on_pool + u - ON_DVE + 1)
                        pool.tensor_tensor(done[:, v, u, :], norm[:, v, u, :], res[:, v, u, :], ALU.add)\
                            .then_inc(s_f, 1)
                alternate(pool, step)

            @block.vector
            def _(dve):
                def weight(t, c):
                    return top_w[:, t, c:c + 1] if isinstance(t, int) else \
                        top_w[:, ds(t, 1), c:c + 1].rearrange("p a b -> p (a b)")

                def scale(i, v):
                    for u in range(ON_DVE):
                        dve.wait_ge(s_nm, i * U + u + 1)
                        dve.tensor_tensor(norm[:, v, u, :], norm[:, v, u, :], gamma[:, :], ALU.mult).then_inc(s_gm, 1)

                def step(i, v, k):
                    count = 16 * (k + 1) if not final(i) else 16 * (k + 2)
                    dve.wait_ge(s_y0[v], count)
                    after(dve, s_nm, (i - 1) * U)
                    for u in range(U):
                        t = i * U + u
                        dve.scalar_tensor_tensor(out=mix[:, v, u, :], in0=y0[:, v, u, :], scalar=weight(t, 0),
                                                 in1=tile_row(token_rows, t), op0=ALU.mult, op1=ALU.add)\
                           .then_inc(s_m0, 1)
                    dve.wait_ge(s_y1[v], count)
                    for u in range(U):
                        t = i * U + u
                        dve.wait_ge(s_m0, t + 1)
                        dve.scalar_tensor_tensor(out=mix[:, v, u, :], in0=y1[:, v, u, :], scalar=weight(t, 1),
                                                 in1=mix[:, v, u, :], op0=ALU.mult, op1=ALU.add).then_inc(s_m1, 1)
                    for u in range(U):
                        dve.wait_ge(s_m1, i * U + u + 1)
                        last = dve.bn_stats(stats[:, u, :], mix[:, v, u, :])
                    last.then_inc(s_bn, 1)
                    dve.wait_ge(s_bn, i + 1)
                    after(dve, s_nm, i * U)
                    settle(dve, turns)
                    for u in range(U):
                        last = dve.bn_aggr(mv[:, u, :], stats[:, u, :])
                    last.then_inc(s_mv, 1)
                    if isinstance(i, int) and i == 0:
                        dve.wait_ge(s_g, 32)
                    else:
                        scale(i - 1, 1 - v)
                    dve.wait_ge(s_sd, i + 1)
                    dve.reciprocal(rstd[:, :], rstd[:, :]).then_inc(s_rc, 1)
                    dve.wait_ge(s_rc, 2 * i + 1)
                    dve.scalar_tensor_tensor(out=nmr[:, :], in0=mv[:, :, 0], scalar=-1.0, in1=rstd[:, :],
                                             op0=ALU.mult, op1=ALU.mult).then_inc(s_rc, 1)
                alternate(dve, step)
                scale(NG - 1, 0)


def tile_row(rows, t, at=0, n=D):
    if isinstance(t, int):
        return rows[:, t, at:at + n]
    return rows[:, ds(t, 1), at:at + n].rearrange("p a d -> p (a d)")


def kernel(**inputs):
    import numpy as np
    import concourse.bacc as bacc
    from concourse.bass_utils import run_bass_kernel_spmd

    a = {k: np.asarray(v) for k, v in inputs.items()}
    pad = NCH * CHUNK - EDGES
    src = np.pad(a["src"], (0, pad), mode="edge").reshape(NCH, P, K)
    dst = np.pad(a["dst"], (0, pad), constant_values=NP - 1).reshape(NCH, P, K).transpose(1, 0, 2)
    attr = np.pad(a["edge_attr_2"], ((0, pad), (0, 0)), mode="edge").reshape(NCH, P, K, 2).transpose(1, 3, 0, 2)
    arrays = {
        "x": np.pad(a["x"], ((0, NP - N), (0, 0))),
        "src": src,
        "dst": dst.reshape(P, NCH * K),
        "attr": attr.reshape(P, 2, NCH * K),
        "w_fwd": a["L0_gnn_W_forward"],
        "w_rev": a["L0_gnn_W_reverse"],
        "w_fwd_t": a["L0_gnn_W_forward"].T,
        "w_rev_t": a["L0_gnn_W_reverse"].T,
        "attn_t": a["L0_gnn_attn_forward"][0].T,
        "gate_w": a["L0_ffn_gate_w"],
        "gate_b": a["L0_ffn_gate_b"],
        "w1": a["L0_ffn_w1"],
        "b1": a["L0_ffn_b1"].reshape(E * FC, P).T,
        "w2": a["L0_ffn_w2"],
        "b2": a["L0_ffn_b2"],
        "gamma": a["L0_ffn_gamma"],
        "beta": a["L0_ffn_beta"],
    }
    nc = bacc.Bacc("TRN2", target_bir_lowering=False, num_devices=1)
    given, feeds = {}, {}
    for name, value in arrays.items():
        value = np.ascontiguousarray(value)
        feeds[f"in_{name}"] = value
        given[name] = nc.dram_tensor(f"in_{name}", value.shape, mybir.dt.from_np(value.dtype),
                                     kind="ExternalInput").ap()
    out = nc.dram_tensor("out", (N, D), F32, kind="ExternalOutput").ap()
    build(nc, **given, out=out)
    r = run_bass_kernel_spmd(nc, [feeds], core_ids=[0])
    return r.results[0]["out"]
```
